# Optimizing a Trainium2 kernel written in Bass

```python
import numpy as np
import jax
import jax.numpy as jnp

def _softmax(x, axis=-1):
    return jax.nn.softmax(x, axis=axis)

def _gelu(x):
    return jax.nn.gelu(x, approximate=True)

def _silu(x):
    return jax.nn.silu(x)

def _sigmoid(x):
    return jax.nn.sigmoid(x)

def _layernorm(x, axis=-1, eps=1e-05):
    m = jnp.mean(x, axis=axis, keepdims=True)
    v = jnp.var(x, axis=axis, keepdims=True)
    return (x - m) / jnp.sqrt(v + eps)

def _scatter_add(tgt, idx, src, axis=0):
    return tgt.at[idx].add(src)

def _segment_sum(src, seg, n):
    return jax.ops.segment_sum(src, seg, n)
kernel_name = 'mk_conv_preact_d2_conv_nhwc256_r4_9e721c'

def setup_inputs(seed: int=0):
    np.random.seed(seed)
    _w = jnp.asarray

    def _rec_inputs():
        import jax
        import jax.numpy as jnp
        _gk = jax.random.key(seed)
        x = -0.000125 + 0.9999 * jax.random.normal(jax.random.fold_in(_gk, 1), (8, 32, 32, 64), jnp.float32)
        return x
    x = _rec_inputs()

    def _L0_conv_setup():
        import jax, jax.numpy as jnp
        import numpy as np
        B, H, W, C = (8, 32, 32, 64)
        K, DT, EPS = (5, 0.2, 0.001)
        LAM2 = 4.0

        def _dwconv(x, w):
            k = w.reshape(3, 3, 1, C)
            return jax.lax.conv_general_dilated(x, k, (1, 1), 'SAME', dimension_numbers=('NHWC', 'HWIO', 'NHWC'), feature_group_count=C)

        def _bn(x, gamma, beta, mean, var):
            return (x - mean) * jax.lax.rsqrt(var + EPS) * gamma + beta

        def _sobel(x):
            xp = jnp.pad(x, ((0, 0), (1, 1), (1, 1), (0, 0)), mode='reflect')
            top, mid, bot = (xp[:, :-2], xp[:, 1:-1], xp[:, 2:])
            gy = bot[:, :, :-2] + 2 * bot[:, :, 1:-1] + bot[:, :, 2:] - (top[:, :, :-2] + 2 * top[:, :, 1:-1] + top[:, :, 2:])
            gx = top[:, :, 2:] + 2 * mid[:, :, 2:] + bot[:, :, 2:] - (top[:, :, :-2] + 2 * mid[:, :, :-2] + bot[:, :, :-2])
            return (gy, gx)
        key = jax.random.key(seed)
        ks = jax.random.split(key, 6)
        f = jnp.float32
        d = {}
        d['s0'] = jax.random.normal(ks[0], (B, H, W, C), f)
        d['wg'] = jax.random.normal(ks[1], (3, 3, C), f) * 0.1
        d['wg1'] = jax.random.normal(ks[2], (3, 3, C), f) * 0.1
        for i, p in enumerate(['g', 'g1', 'out']):
            k4 = jax.random.split(ks[3 + i], 4)
            d[p + '_gamma'] = 1.0 + 0.1 * jax.random.normal(k4[0], (C,), f)
            d[p + '_beta'] = 0.1 * jax.random.normal(k4[1], (C,), f)
            d[p + '_mean'] = 0.1 * jax.random.normal(k4[2], (C,), f)
            d[p + '_var'] = 0.5 + jax.random.uniform(k4[3], (C,), f)
        return d
    _L0_conv_all = _L0_conv_setup()
    _L0_conv_in = {k: v for k, v in _L0_conv_all.items() if k in ('wg', 'wg1', 'g_gamma', 'g_beta', 'g_mean', 'g_var', 'g1_gamma', 'g1_beta', 'g1_mean', 'g1_var', 'out_gamma', 'out_beta', 'out_mean', 'out_var')}
    del _L0_conv_all

    def _L1_conv_setup():
        import jax, jax.numpy as jnp
        from jax import lax
        import numpy as np
        K = 3
        DG = 1
        PAD = 1

        def _dcn_forward(x, w_offset, b_offset, filt):
            B, H, W, C = x.shape
            F = filt.shape[0]
            KK = K * K
            Cg = C // DG
            HW = H * W
            wi = lax.conv_general_dilated(x, w_offset, window_strides=(1, 1), padding='SAME', dimension_numbers=('NHWC', 'HWIO', 'NHWC')) + b_offset
            wi = jnp.transpose(wi, (0, 3, 1, 2))
            o1, o2, m = jnp.split(wi, 3, axis=1)
            mask = jax.nn.sigmoid(m).reshape(B, DG, KK, 1, HW)
            ki, kj = jnp.divmod(jnp.arange(KK), K)
            base_y = (jnp.arange(H)[None, :, None] - PAD + ki[:, None, None]).astype(jnp.float32)
            base_x = (jnp.arange(W)[None, None, :] - PAD + kj[:, None, None]).astype(jnp.float32)
            py = o1.reshape(B, DG, KK, H, W) + base_y[None, None]
            px = o2.reshape(B, DG, KK, H, W) + base_x[None, None]
            y0f = jnp.floor(py)
            x0f = jnp.floor(px)
            dy = (py - y0f).reshape(B, DG, KK, 1, HW)
            dx = (px - x0f).reshape(B, DG, KK, 1, HW)
            y0 = y0f.astype(jnp.int32)
            x0 = x0f.astype(jnp.int32)
            xg = x.reshape(B, HW, DG, Cg).transpose(0, 2, 3, 1)

            def gather(yi, xi):
                valid = (yi >= 0) & (yi < H) & (xi >= 0) & (xi < W)
                yc = jnp.clip(yi, 0, H - 1)
                xc = jnp.clip(xi, 0, W - 1)
                idx = (yc * W + xc).reshape(B, DG, KK, 1, HW)
                v = jnp.take_along_axis(xg[:, :, None, :, :], idx, axis=-1)
                return v * valid.reshape(B, DG, KK, 1, HW).astype(x.dtype)
            v00 = gather(y0, x0)
            v01 = gather(y0, x0 + 1)
            v10 = gather(y0 + 1, x0)
            v11 = gather(y0 + 1, x0 + 1)
            sampled = (v00 * (1 - dy) * (1 - dx) + v01 * (1 - dy) * dx + v10 * dy * (1 - dx) + v11 * dy * dx) * mask
            col = sampled.transpose(0, 2, 1, 3, 4).reshape(B, KK, C, HW)
            w = filt.reshape(F, C, KK)
            out = jnp.einsum('bkcp,fck->bfp', col, w).reshape(B, F, H, W)
            return jnp.transpose(out, (0, 2, 3, 1))
        key = jax.random.key(seed)
        k1, k2, k3 = jax.random.split(key, 3)
        B, H, W, C, F = (4, 16, 16, 64, 64)
        x = jax.random.normal(k1, (B, H, W, C), jnp.float32)
        w_offset = jax.random.normal(k2, (K, K, C, DG * 3 * K * K), jnp.float32) * 0.01
        b_offset = jnp.zeros((DG * 3 * K * K,), jnp.float32)
        filt = jax.random.normal(k3, (F, C, K, K), jnp.float32) * 0.05
        return {'x': x, 'w_offset': w_offset, 'b_offset': b_offset, 'filt': filt}
    _L1_conv_all = _L1_conv_setup()
    _L1_conv_in = {k: v for k, v in _L1_conv_all.items() if k in ('w_offset', 'b_offset', 'filt')}
    del _L1_conv_all
    return {'x': x, 'L0_conv_wg': _L0_conv_in['wg'], 'L0_conv_wg1': _L0_conv_in['wg1'], 'L0_conv_g_gamma': _L0_conv_in['g_gamma'], 'L0_conv_g_beta': _L0_conv_in['g_beta'], 'L0_conv_g_mean': _L0_conv_in['g_mean'], 'L0_conv_g_var': _L0_conv_in['g_var'], 'L0_conv_g1_gamma': _L0_conv_in['g1_gamma'], 'L0_conv_g1_beta': _L0_conv_in['g1_beta'], 'L0_conv_g1_mean': _L0_conv_in['g1_mean'], 'L0_conv_g1_var': _L0_conv_in['g1_var'], 'L0_conv_out_gamma': _L0_conv_in['out_gamma'], 'L0_conv_out_beta': _L0_conv_in['out_beta'], 'L0_conv_out_mean': _L0_conv_in['out_mean'], 'L0_conv_out_var': _L0_conv_in['out_var'], 'L1_conv_w_offset': _L1_conv_in['w_offset'], 'L1_conv_b_offset': _L1_conv_in['b_offset'], 'L1_conv_filt': _L1_conv_in['filt']}

def reference(x, L0_conv_wg, L0_conv_wg1, L0_conv_g_gamma, L0_conv_g_beta, L0_conv_g_mean, L0_conv_g_var, L0_conv_g1_gamma, L0_conv_g1_beta, L0_conv_g1_mean, L0_conv_g1_var, L0_conv_out_gamma, L0_conv_out_beta, L0_conv_out_mean, L0_conv_out_var, L1_conv_w_offset, L1_conv_b_offset, L1_conv_filt):
    import jax
    import jax.numpy as jnp

    def _L0_conv_ref(s0, wg, wg1, g_gamma, g_beta, g_mean, g_var, g1_gamma, g1_beta, g1_mean, g1_var, out_gamma, out_beta, out_mean, out_var):
        import jax, jax.numpy as jnp
        import numpy as np
        B, H, W, C = (8, 32, 32, 64)
        K, DT, EPS = (5, 0.2, 0.001)
        LAM2 = 4.0

        def _dwconv(x, w):
            k = w.reshape(3, 3, 1, C)
            return jax.lax.conv_general_dilated(x, k, (1, 1), 'SAME', dimension_numbers=('NHWC', 'HWIO', 'NHWC'), feature_group_count=C)

        def _bn(x, gamma, beta, mean, var):
            return (x - mean) * jax.lax.rsqrt(var + EPS) * gamma + beta

        def _sobel(x):
            xp = jnp.pad(x, ((0, 0), (1, 1), (1, 1), (0, 0)), mode='reflect')
            top, mid, bot = (xp[:, :-2], xp[:, 1:-1], xp[:, 2:])
            gy = bot[:, :, :-2] + 2 * bot[:, :, 1:-1] + bot[:, :, 2:] - (top[:, :, :-2] + 2 * top[:, :, 1:-1] + top[:, :, 2:])
            gx = top[:, :, 2:] + 2 * mid[:, :, 2:] + bot[:, :, 2:] - (top[:, :, :-2] + 2 * mid[:, :, :-2] + bot[:, :, :-2])
            return (gy, gx)
        fsrc = s0
        h = s0
        h0 = fsrc
        g = jax.nn.relu(_bn(_dwconv(h, wg), g_gamma, g_beta, g_mean, g_var))
        g1 = jax.nn.relu(_bn(_dwconv(h, wg1), g1_gamma, g1_beta, g1_mean, g1_var))
        gy, gx = _sobel(h)
        Dx = 1.0 / (gy * gy / LAM2 + 1.0)
        Dy = 1.0 / (gx * gx / LAM2 + 1.0)
        ux = 0.5 * (jnp.roll(g, 1, axis=2) - jnp.roll(g, -1, axis=2))
        vy = 0.5 * (jnp.roll(g1, 1, axis=3) - jnp.roll(g1, -1, axis=3))
        Ax, Ay = (g * DT, g1 * DT)
        Bx, By = (Dx * DT, Dy * DT)
        E = (ux + vy) * DT
        D = 1.0 / (1.0 + 2.0 * Bx + 2.0 * By)
        cm_x, cp_x = (-Ax + 2.0 * Bx, Ax + 2.0 * Bx)
        cm_y, cp_y = (-Ay + 2.0 * By, Ay + 2.0 * By)
        c0 = 1.0 - 2.0 * Bx - 2.0 * By
        for _ in range(K):
            prev = h
            h = D * (c0 * h0 - 2.0 * E * h + cm_x * jnp.roll(h, 1, axis=2) + cp_x * jnp.roll(h, -1, axis=2) + cm_y * jnp.roll(h, 1, axis=3) + cp_y * jnp.roll(h, -1, axis=3))
            h = h + D * (2.0 * DT) * fsrc
            h0 = prev
        return jax.nn.relu(_bn(h, out_gamma, out_beta, out_mean, out_var))

    def _L1_conv_ref(x, w_offset, b_offset, filt):
        import jax, jax.numpy as jnp
        from jax import lax
        import numpy as np
        K = 3
        DG = 1
        PAD = 1

        def _dcn_forward(x, w_offset, b_offset, filt):
            B, H, W, C = x.shape
            F = filt.shape[0]
            KK = K * K
            Cg = C // DG
            HW = H * W
            wi = lax.conv_general_dilated(x, w_offset, window_strides=(1, 1), padding='SAME', dimension_numbers=('NHWC', 'HWIO', 'NHWC')) + b_offset
            wi = jnp.transpose(wi, (0, 3, 1, 2))
            o1, o2, m = jnp.split(wi, 3, axis=1)
            mask = jax.nn.sigmoid(m).reshape(B, DG, KK, 1, HW)
            ki, kj = jnp.divmod(jnp.arange(KK), K)
            base_y = (jnp.arange(H)[None, :, None] - PAD + ki[:, None, None]).astype(jnp.float32)
            base_x = (jnp.arange(W)[None, None, :] - PAD + kj[:, None, None]).astype(jnp.float32)
            py = o1.reshape(B, DG, KK, H, W) + base_y[None, None]
            px = o2.reshape(B, DG, KK, H, W) + base_x[None, None]
            y0f = jnp.floor(py)
            x0f = jnp.floor(px)
            dy = (py - y0f).reshape(B, DG, KK, 1, HW)
            dx = (px - x0f).reshape(B, DG, KK, 1, HW)
            y0 = y0f.astype(jnp.int32)
            x0 = x0f.astype(jnp.int32)
            xg = x.reshape(B, HW, DG, Cg).transpose(0, 2, 3, 1)

            def gather(yi, xi):
                valid = (yi >= 0) & (yi < H) & (xi >= 0) & (xi < W)
                yc = jnp.clip(yi, 0, H - 1)
                xc = jnp.clip(xi, 0, W - 1)
                idx = (yc * W + xc).reshape(B, DG, KK, 1, HW)
                v = jnp.take_along_axis(xg[:, :, None, :, :], idx, axis=-1)
                return v * valid.reshape(B, DG, KK, 1, HW).astype(x.dtype)
            v00 = gather(y0, x0)
            v01 = gather(y0, x0 + 1)
            v10 = gather(y0 + 1, x0)
            v11 = gather(y0 + 1, x0 + 1)
            sampled = (v00 * (1 - dy) * (1 - dx) + v01 * (1 - dy) * dx + v10 * dy * (1 - dx) + v11 * dy * dx) * mask
            col = sampled.transpose(0, 2, 1, 3, 4).reshape(B, KK, C, HW)
            w = filt.reshape(F, C, KK)
            out = jnp.einsum('bkcp,fck->bfp', col, w).reshape(B, F, H, W)
            return jnp.transpose(out, (0, 2, 3, 1))
        return _dcn_forward(x, w_offset, b_offset, filt)

    def _gn(v, G=32, eps=1e-05):
        B_, H_, W_, C_ = v.shape
        g = v.reshape(B_, H_, W_, G, C_ // G)
        m = jnp.mean(g, axis=(1, 2, 4), keepdims=True)
        s = jnp.var(g, axis=(1, 2, 4), keepdims=True)
        return ((g - m) / jnp.sqrt(s + eps)).reshape(v.shape)

    def _ln_c(v, eps=1e-06):
        m = jnp.mean(v, axis=-1, keepdims=True)
        s = jnp.var(v, axis=-1, keepdims=True)
        return (v - m) / jnp.sqrt(s + eps)

    def _ln_t(v, eps=1e-05):
        m = jnp.mean(v, axis=-1, keepdims=True)
        s = jnp.var(v, axis=-1, keepdims=True)
        return (v - m) / jnp.sqrt(s + eps)

    def _to_tokens(v):
        B_, H_, W_, C_ = v.shape
        return v.reshape(B_, H_ * W_, C_)

    def _from_tokens(t, like):
        return t.reshape(like.shape)
    x = x + _L0_conv_ref(_gn(x), L0_conv_wg, L0_conv_wg1, L0_conv_g_gamma, L0_conv_g_beta, L0_conv_g_mean, L0_conv_g_var, L0_conv_g1_gamma, L0_conv_g1_beta, L0_conv_g1_mean, L0_conv_g1_var, L0_conv_out_gamma, L0_conv_out_beta, L0_conv_out_mean, L0_conv_out_var)
    x = x + _L1_conv_ref(_gn(x), L1_conv_w_offset, L1_conv_b_offset, L1_conv_filt)
    return x

_drawn_inputs = setup_inputs


def setup_inputs(seed=0):
    import zlib

    import numpy as np

    out = dict(_drawn_inputs(seed))
    spreads = {'L1_conv_b_offset': (0.0, 0.1)}
    factors = {'L0_conv_g_gamma': 7.932,
     'L0_conv_g_beta': 3.706,
     'L0_conv_g_mean': 3.271,
     'L0_conv_g_var': 4.52,
     'L0_conv_g1_gamma': 8.0,
     'L0_conv_g1_beta': 3.37,
     'L0_conv_g1_mean': 2.892,
     'L0_conv_g1_var': 6.418}
    for name, (base, spread) in spreads.items():
        noise = np.random.default_rng([zlib.crc32(name.encode()), seed]).standard_normal(out[name].shape)
        drawn = base * np.exp(spread * noise) if base else spread * noise
        out[name] = jnp.asarray(drawn.astype(out[name].dtype))
    for name, factor in factors.items():
        out[name] = (out[name] * factor).astype(out[name].dtype)
    return out
```

```python
import concourse.bass as bass
from concourse import mybir
from contextlib import ExitStack
import numpy as np

B, H, W, C = 8, 32, 32, 64
P = 128
IMGS = P // H
TILES = B // IMGS
WC = W * C
GROUP_SIZE = 2
GROUPS = C // GROUP_SIZE
K2 = 9
OFFS = 3 * K2
DT, BN_EPS, GN_EPS = 0.2, 0.001, 1e-05
STEPS = 5
LO = 2
TY = TX = H + LO + 1
ENTRY = 4 * C
ENTRIES = B * TY * TX
CLIP_LOW, CLIP_HIGH = -float(LO), H + 0.5
BANK = 512
NBANK = WC // BANK
CHUNK_W = BANK // C
PAIRS = W // 2
PAIRS_BANK = PAIRS // NBANK
PLAN = ([("turn", q, "act") for q in range(NBANK)] + [("diff", q, "act") for q in range(NBANK)]
        + [("smooth", q, "act") for q in range(NBANK)] + [("conv", q, "dve") for q in range(2 * NBANK)]
        + [("own", q, "dve") for q in range(NBANK)] + [("pde", q, "dve") for q in range(STEPS * NBANK)]
        + [("turn2", q, "act") for q in range(NBANK)]
        + [("off", 0, "act"), ("off", 1, "act"), ("offback", 0, "dve"), ("off", 2, "act"), ("offback", 1, "dve"),
           ("off", 3, "act"), ("offback", 2, "dve"), ("offback", 3, "dve")])
N_ALL = len(PLAN)
AT = {(what, q): n for n, (what, q, _) in enumerate(PLAN)}
QUARTERS = NBANK
QCOLS = W // QUARTERS
OFFP = 32
COLS = 4
GATHER_GROUPS = W // COLS
PARTS = 3
PART = K2 // PARTS
PART_SLOTS = 3
PRODS = 5
SLOTS = 6
C_EYE, C_ONES, C_DIFF, C_SMOOTH, C_MASK, C_NEG, C_BASE = 0, 128, 256, 384, 512, 576, 704
C_ENT = C_BASE + W * 2 * K2
C_ALL = C_ENT + TILES
N_STAGES = 9


def build_program(nc, x_in, taps_in, offw_in, filt_in, bn_in, offb_in, const_in, out_dram):
    f32, i32, u32 = mybir.dt.float32, mybir.dt.int32, mybir.dt.uint32
    ALU, ACT, AX = mybir.AluOpType, mybir.ActivationFunctionType, mybir.AxisListType
    table = nc.dram_tensor("table", [ENTRIES, ENTRY], f32, kind="Internal").ap()
    table_y = table.rearrange("(b y x) e -> b y x e", b=B, y=TY)

    with ExitStack() as ctx:
        def sb(name, shape, dt=f32):
            return ctx.enter_context(nc.sbuf_tensor(name, shape, dt))

        def psum(name, shape):
            return ctx.enter_context(nc.psum_tensor(name, shape, f32))

        def sem(name):
            return ctx.enter_context(nc.semaphore(name))

        const = sb("const", [P, C_ALL])
        eye = const[:, C_EYE:C_EYE + P]
        ones_block = const[:, C_ONES:C_ONES + P]
        diff_h = const[:, C_DIFF:C_DIFF + P]
        smooth_h = const[:, C_SMOOTH:C_SMOOTH + P]
        minus_eye = const[:, C_NEG:C_NEG + P]
        same_c = const[:, C_MASK:C_MASK + C]
        base_pos = const[:, C_BASE:C_ENT].rearrange("p (w o) -> p w o", o=2 * K2)
        taps = sb("taps", [P, 3, 4, 2])
        conv_w = sb("conv_w", [P, 3, 4, 2 * C])
        off_w = sb("off_w", [P, 3, 3, 2 * OFFP])
        filt = sb("filt", [P, K2, C])
        off_b = sb("off_b", [P, OFFS])
        bn = sb("bn", [P, 4, 3, C])
        bn_scale = sb("bn_scale", [P, 3, C])
        bn_shift = sb("bn_shift", [P, 3, C])
        x1 = [sb(f"x1_{t}", [P, WC]) for t in range(TILES)]
        h_pad = [sb(f"h_pad{i}", [P, W + 2, C + 2]) for i in range(2)]
        scratch = sb("scratch", [P, (W + 2) * (C + 2)])
        xn_flat = scratch[:, 0:WC]
        gx_pad = scratch[:, :].rearrange("p (w c) -> p w c", c=C + 2)
        xn_pad = scratch[:, 0:(W + 2) * C].rearrange("p (w c) -> p w c", c=C)
        xT_mid = sb("xT_mid", [P, WC])
        shared = sb("shared", [P, 2 * WC])
        xT = (shared[:, 0:WC], xT_mid[:, :], shared[:, WC:2 * WC])
        arr = [sb(f"arr{i}", [P, WC]) for i in range(7)]
        prod = shared[:, 0:SLOTS * BANK].rearrange("p (s n) -> p s n", n=BANK)
        rest = shared[:, SLOTS * BANK:(SLOTS + 2) * BANK].rearrange("p (s n) -> p s n", n=BANK)
        rsum = sb("rsum", [P, C])
        gmean = sb("gmean", [P, GROUPS])
        gvar = sb("gvar", [P, GROUPS])
        grstd = sb("grstd", [P, GROUPS])
        gtmp = sb("gtmp", [P, GROUPS])
        one = sb("one", [P, 1])
        pos_int = sb("pos_int", [P, W * 2 * K2], i32)
        corner_w = sb("corner_w", [P, TILES, W, K2 * 4])
        index = sb("index", [P, TILES * W * K2], u32)
        index_now = sb("index_now", [P, 2, COLS, K2], u32)
        pixels = sb("pixels", [P, COLS, K2, ENTRY])
        sampled_T = sb("sampled_T", [P, 2, K2 * P])
        acc = psum("acc", [P, NBANK, BANK])
        turned = psum("turned", [P, PART_SLOTS, BANK])
        misc = psum("misc", [P, BANK])
        out_ps = misc[:, 0:COLS * C]
        stat_ps = misc[:, COLS * C:COLS * C + C]

        s_const, s_taps, s_offw, s_filt, s_bn, s_offb = (
            sem(n) for n in ("const_in", "taps_in", "offw_in", "filt_in", "bn_in", "offb_in"))
        s_x = [sem(f"x_in{t}") for t in range(TILES)]
        s_zeros = sem("zeros_ready")
        s_cleared = sem("table_cleared")
        s_table = sem("table_written")
        s_conv_w = sem("conv_w_ready")
        s_bn_ve = sem("bn_var_eps_ready")
        s_bn_sd = sem("bn_sd_ready")
        s_rsum = sem("row_sums_ready")
        s_stat = sem("group_sums_ready")
        s_centred = sem("centred_ready")
        s_square = sem("squares_ready")
        s_ve = sem("var_eps_ready")
        s_sd = sem("sd_ready")
        s_xn = sem("xn_ready")
        s_halo = sem("xn_halo_ready")
        s_bank = sem("bank_full")
        s_act = sem("bank_emptied_by_act")
        s_dve = sem("bank_emptied_by_dve")
        s_grad = sem("gradients_ready")
        s_grad2 = sem("squared_gradients_ready")
        s_den = sem("denominator_ready")
        s_seed = sem("reciprocal_seed_ready")
        s_pq = sem("p_plus_q_ready")
        s_c0 = sem("c0_ready")
        s_gates = sem("gates_ready")
        s_prod = sem("product_ready")
        s_summed = sem("product_summed")
        s_hhalo = sem("h_halo_ready")
        s_xn2 = sem("xn2_ready")
        s_mask = sem("mask_ready")
        s_index = sem("index_ready")
        s_copied = sem("indices_copied")
        s_begun = sem("column_begun")
        s_pixels = [sem(f"pixels_in{j}") for j in range(COLS)]
        s_halved = sem("halved_ready")
        s_part = sem("part_turned")
        s_sT = sem("sampled_T_ready")
        s_weighted = sem("weighted")
        s_out = sem("column_filtered")
        s_x2 = sem("group_added")
        s_store = sem("stored")
        s_v = sem("vector_step")
        s_a = sem("scalar_step")

        block = ctx.enter_context(nc.Block())

        def flat(a):
            return a.rearrange("p w c -> p (w c)")

        def wc(a):
            return a.rearrange("p (w c) -> p w c", c=C)

        def inner(a):
            return a[:, 1:W + 1, 1:C + 1]

        def emptied(t, what, q):
            n = AT[what, q]
            who = PLAN[n][2]
            mine = [p[2] for p in PLAN].count(who)
            return {"act": s_act, "dve": s_dve}[who], t * mine + [p[2] for p in PLAN[:n + 1]].count(who)

        def full(t, what, q):
            return t * N_ALL + AT[what, q] + 1

        def bank(what, q):
            return acc[:, AT[what, q] % NBANK, :]

        def wait_bank_empty(pe, t, what, q):
            m = t * N_ALL + AT[what, q] - NBANK
            if m >= 0:
                pe.wait_ge(*emptied(m // N_ALL, *PLAN[m % N_ALL][:2]))

        def interleave(stage, group, groups_loop):
            for k in range(N_STAGES):
                stage(0, k)
            for g in range(GATHER_GROUPS):
                stage(1, g)
                if g == GATHER_GROUPS - 1:
                    stage(1, N_STAGES - 1)
                group(0, g)
            groups_loop(1)

        @block.sync
        def _(sp):
            sp.dma_start(x1[0][:, :], x_in[0:P, :]).then_inc(s_x[0], 16)
            sp.dma_start(const[:, :], const_in).then_inc(s_const, 16)
            sp.dma_start(bn[:, :, :, :].rearrange("p a b c -> p (a b c)"),
                         bn_in.to_broadcast([P, 12 * C])).then_inc(s_bn, 16)
            sp.dma_start(taps[:, :, :, :].rearrange("p a b c -> p (a b c)"), taps_in).then_inc(s_taps, 16)
            sp.dma_start(off_w[:, :, :, :].rearrange("p a b c -> p (a b c)"), offw_in).then_inc(s_offw, 16)
            for half in range(2):
                sp.dma_start(filt[half * C:(half + 1) * C, :, :].rearrange("p k f -> p (k f)"), filt_in)\
                  .then_inc(s_filt, 16)
            sp.dma_start(off_b[:, :], offb_in.to_broadcast([P, OFFS])).then_inc(s_offb, 16)
            sp.dma_start(x1[1][:, :], x_in[P:2 * P, :]).then_inc(s_x[1], 16)
            sp.wait_ge(s_zeros, 1)
            for b in range(B):
                sp.dma_start(table[b * TY * TX:(b + 1) * TY * TX, :].rearrange("(y x) e -> y x e", y=TY),
                             corner_w[0:TY, :, :, :].rearrange("p t w k -> p (t w k)")[:, 0:ENTRY]
                             .unsqueeze(1).to_broadcast([TY, TX, ENTRY])).then_inc(s_cleared, 16)
            sp.wait_ge(s_cleared, 16 * B)
            for t in range(TILES):
                sp.wait_ge(s_xn2, t + 1)
                for i in range(IMGS):
                    rows = scratch[i * H:(i + 1) * H, 0:(W + 1) * C].rearrange("p (w c) -> p w c", c=C)
                    pairs = bass.AP(tensor=rows.tensor, offset=rows.offset,
                                    ap=[list(rows.ap[0]), [C, W + 1], [1, 2 * C]])
                    for half in range(2):
                        sp.dma_start(table_y[t * IMGS + i, LO - half:LO - half + H, 1:W + 2,
                                             half * 2 * C:(half + 1) * 2 * C], pairs).then_inc(s_table, 16)
            for t in range(TILES):
                with sp.Fori(0, GATHER_GROUPS, 1) as g:
                    sp.wait_ge(s_x2, g + (t * GATHER_GROUPS + 1))
                    sp.dma_start(out_dram[t * P:(t + 1) * P, bass.ds(g * (COLS * C), COLS * C)],
                                 x1[t][:, bass.ds(g * (COLS * C), COLS * C)]).then_inc(s_store, 16)
            sp.wait_ge(s_store, 16 * TILES * GATHER_GROUPS)

        @block.gpsimd
        def _(pool):
            for t in range(TILES):
                pool.wait_ge(s_table, 16 * 2 * IMGS * (t + 1))
                with pool.Fori(0, QUARTERS, 1) as i:
                    pool.wait_ge(s_index, i + (t * QUARTERS + 1))
                    for half in range(2):
                        first = i * 2 + (t * GATHER_GROUPS + half)
                        pool.tensor_copy(index_now[:, half, :, :].rearrange("p j k -> p (j k)"),
                                         index[:, bass.ds(first * (COLS * K2), COLS * K2)]).then_inc(s_copied, 1)
                        pool.wait_ge(s_copied, first + 1)
                        for j in range(COLS):
                            pool.wait_ge(s_part, first * (COLS * PARTS) + (j + 1) * PARTS)
                            pool.sem_inc(s_begun, 1)
                            for k in range(K2):
                                pool.indirect_dma_start(
                                    out=pixels[:, j, k, :], out_offset=None, in_=table,
                                    in_offset=bass.IndirectOffsetOnAxis(ap=index_now[:, half, j, k:k + 1], axis=0),
                                ).then_inc(s_pixels[j], 16)


        @block.vector
        def _(dve):
            steps = [0]

            def seq(ins):
                steps[0] += 1
                ins.then_inc(s_v, 1)
                dve.wait_ge(s_v, steps[0])

            def per_group(a):
                return a[:, :].unsqueeze(1).unsqueeze(3).to_broadcast([P, W, GROUPS, GROUP_SIZE])

            def grouped(a):
                return a.rearrange("p w (g j) -> p w g j", j=GROUP_SIZE)

            def rsqrt_refined(root, v, tmp):
                seq(dve.reciprocal(root, root))
                seq(dve.tensor_tensor(tmp, root, root, ALU.mult))
                seq(dve.tensor_tensor(tmp, tmp, v, ALU.mult))
                seq(dve.tensor_scalar(tmp, tmp, -0.5, 1.5, ALU.mult, ALU.add))
                seq(dve.tensor_tensor(root, root, tmp, ALU.mult))

            def group_norm(k, src, dst, square, ready):
                dve.tensor_reduce(rsum[:, :], src.rearrange("p w c -> p c w"), AX.X, ALU.add).then_inc(s_rsum, 1)
                dve.wait_ge(s_stat, 2 * k + 1)
                seq(dve.tensor_reduce(gmean[:, :], stat_ps.rearrange("p (g j) -> p g j", j=GROUP_SIZE), AX.X, ALU.add))
                seq(dve.tensor_scalar(gmean[:, :], gmean[:, :], 1.0 / (H * W * GROUP_SIZE), None, ALU.mult))
                dve.tensor_tensor(grouped(dst), grouped(src), per_group(gmean), ALU.subtract).then_inc(s_centred, 1)
                dve.wait_ge(s_square, k + 1)
                dve.tensor_reduce(rsum[:, :], square.rearrange("p (w c) -> p c w", c=C), AX.X, ALU.add)\
                   .then_inc(s_rsum, 1)
                dve.wait_ge(s_stat, 2 * k + 2)
                seq(dve.tensor_reduce(gvar[:, :], stat_ps.rearrange("p (g j) -> p g j", j=GROUP_SIZE), AX.X, ALU.add))
                dve.tensor_scalar(gvar[:, :], gvar[:, :], 1.0 / (H * W * GROUP_SIZE), GN_EPS, ALU.mult, ALU.add)\
                   .then_inc(s_ve, 1)
                dve.wait_ge(s_sd, k + 1)
                rsqrt_refined(grstd[:, :], gvar[:, :], gtmp[:, :])
                dve.tensor_tensor(grouped(dst), grouped(dst), per_group(grstd), ALU.mult).then_inc(ready, 1)

            def parameters():
                dve.wait_ge(s_bn, 16)
                gamma, beta, mean, var = (bn[:, i, :, :] for i in range(4))
                dve.tensor_scalar(var, var, BN_EPS, None, ALU.add).then_inc(s_bn_ve, 1)
                dve.wait_ge(s_bn_sd, 1)
                rsqrt_refined(bn_scale[:, :, :], var, bn_shift[:, :, :])
                seq(dve.tensor_tensor(bn_scale[:, :, :], bn_scale[:, :, :], gamma, ALU.mult))
                seq(dve.tensor_tensor(bn_shift[:, :, :], bn_scale[:, :, :], mean, ALU.mult))
                seq(dve.tensor_tensor(bn_shift[:, :, :], beta, bn_shift[:, :, :], ALU.subtract))
                seq(dve.tensor_scalar(bn_scale[:, 0:2, :], bn_scale[:, 0:2, :], DT, None, ALU.mult))
                seq(dve.tensor_scalar(bn_shift[:, 0:2, :], bn_shift[:, 0:2, :], DT, None, ALU.mult))
                dve.wait_ge(s_const, 16)
                dve.wait_ge(s_taps, 16)
                cells = conv_w[:, :, :, :].rearrange("p a b (g c) -> p (a b g) c", c=C)
                seq(dve.tensor_tensor(cells, same_c.unsqueeze(1).to_broadcast([P, 24, C]),
                                      taps[:, :, :, :].rearrange("p a b g -> p (a b g)").unsqueeze(2)
                                      .to_broadcast([P, 24, C]), ALU.mult))
                rows = conv_w[:, :, :, :].rearrange("p a b c -> p (a b) c")
                dve.tensor_tensor(rows, rows, bn_scale[:, 0:2, :].rearrange("p g c -> p (g c)").unsqueeze(1)
                                  .to_broadcast([P, 12, 2 * C]), ALU.mult).then_inc(s_conv_w, 1)

            def sobel(t):
                u, v, gy, gx = (wc(arr[i][:, :]) for i in range(4))
                dve.wait_ge(*emptied(t, "diff", NBANK - 1))
                seq(dve.tensor_tensor(gy[:, 1:W - 1, :], u[:, 0:W - 2, :], u[:, 2:W, :], ALU.add))
                seq(dve.tensor_scalar(gy[:, 0, :], u[:, 1, :], 2.0, None, ALU.mult))
                seq(dve.tensor_scalar(gy[:, W - 1, :], u[:, W - 2, :], 2.0, None, ALU.mult))
                dve.scalar_tensor_tensor(arr[2][:, :], arr[0][:, :], 2.0, arr[2][:, :], ALU.mult, ALU.add)\
                   .then_inc(s_grad, 1)
                dve.wait_ge(*emptied(t, "smooth", NBANK - 1))
                seq(dve.memset(gx[:, 0, :], 0.0))
                seq(dve.memset(gx[:, W - 1, :], 0.0))
                dve.tensor_tensor(gx[:, 1:W - 1, :], v[:, 2:W, :], v[:, 0:W - 2, :], ALU.subtract).then_inc(s_grad, 1)

            def diffusion(t):
                A, Bq = arr[2][:, :], arr[3][:, :]
                den, r = arr[0][:, :], arr[1][:, :]
                dve.wait_ge(s_grad2, 2 * t + 2)
                seq(dve.scalar_tensor_tensor(den, A, 1.0, Bq, ALU.add, ALU.mult))
                seq(dve.scalar_tensor_tensor(r, A, 3.5, Bq, ALU.mult, ALU.add))
                seq(dve.scalar_tensor_tensor(den, den, 2.5, r, ALU.mult, ALU.add))
                dve.tensor_scalar(den, den, 4.5, None, ALU.add).then_inc(s_den, 1)
                dve.wait_ge(s_seed, t + 1)
                seq(dve.tensor_tensor(den, den, r, ALU.mult))
                seq(dve.scalar_tensor_tensor(r, den, 2.0, r, ALU.subtract, ALU.mult, reverse0=True))
                seq(dve.scalar_tensor_tensor(Bq, Bq, 1.0, r, ALU.add, ALU.mult))
                seq(dve.scalar_tensor_tensor(A, A, 1.0, r, ALU.add, ALU.mult))
                dve.tensor_tensor(arr[0][:, :], A, Bq, ALU.add).then_inc(s_pq, 1)
                dve.wait_ge(s_pq, t + 1)
                seq(dve.tensor_scalar(arr[1][:, :], arr[0][:, :], -1.0, 1.0, ALU.mult, ALU.add))
                seq(dve.scalar_tensor_tensor(wc(arr[5][:, :]), wc(arr[1][:, :]), 2.0 * DT, wc(xn_flat),
                                             ALU.mult, ALU.mult))

            def gate_banks(t, first):
                for q in range(first, first + NBANK):
                    dve.wait_ge(s_bank, full(t, "conv", q))
                    both = bank("conv", q).rearrange("p (w g c) -> p w g c", g=2, c=C)
                    for g, dst in enumerate((gx_pad, h_pad[1])):
                        cols = both.shape[1]
                        ins = dve.tensor_tensor(
                            dst[:, 1 + q * cols:1 + (q + 1) * cols, 1:C + 1], both[:, :, g, :],
                            bn_shift[:, g, :].unsqueeze(1).to_broadcast([P, cols, C]), ALU.add)
                        if g == 1:
                            ins.then_inc(s_dve, 1)

            def transport(t):
                D, DAx = arr[1][:, :], arr[0][:, :]
                ay = h_pad[1]
                dve.wait_ge(s_gates, 2 * t + 1)
                dve.wait_ge(s_c0, t + 1)
                seq(dve.tensor_tensor(wc(DAx), wc(D), inner(gx_pad), ALU.mult))
                seq(dve.tensor_tensor(arr[3][:, :], arr[3][:, :], DAx, ALU.subtract))
                seq(dve.scalar_tensor_tensor(DAx, DAx, 2.0, arr[3][:, :], ALU.mult, ALU.add))
                dve.wait_ge(s_gates, 2 * t + 2)
                for q in range(NBANK):
                    dve.wait_ge(s_bank, full(t, "own", q))
                    cols = slice(q * BANK, (q + 1) * BANK)
                    dve.tensor_tensor(arr[6][:, cols], bank("own", q), D[:, cols], ALU.mult).then_inc(s_dve, 1)
                dve.wait_ge(*emptied(t, "own", NBANK - 1))
                seq(dve.tensor_tensor(wc(D), wc(D), inner(ay), ALU.mult))
                seq(dve.tensor_tensor(arr[2][:, :], arr[2][:, :], D, ALU.subtract))
                seq(dve.scalar_tensor_tensor(D, D, 2.0, arr[2][:, :], ALU.mult, ALU.add))

            def chunk_products(t, it, q):
                n = (t * STEPS + it) * NBANK + q
                h, h0 = h_pad[it % 2], h_pad[0 if it == 0 else (it + 1) % 2]
                c = (it + q) % NBANK
                a, b = c * CHUNK_W, (c + 1) * CHUNK_W
                flat_cols = slice(c * BANK, (c + 1) * BANK)
                kept = rest[:, n % 2, :].rearrange("p (w c) -> p w c", c=C)
                k = it * NBANK + q
                if k >= 2:
                    dve.wait_ge(*emptied(t, "pde", k - 2))
                seq(dve.tensor_tensor(kept, wc(arr[4][:, :])[:, a:b, :], h0[:, a + 1:b + 1, 1:C + 1], ALU.mult))
                seq(dve.tensor_tensor(rest[:, n % 2, :], rest[:, n % 2, :], arr[5][:, flat_cols], ALU.add))
                if it:
                    dve.wait_ge(s_hhalo, (t * (STEPS - 1) + it - 1) * NBANK + (3 if q == 0 else 4))
                for j, (coef, w0, c0) in enumerate(((6, 1, 1), (2, 1, 0), (1, 1, 2), (3, 0, 1), (0, 2, 1))):
                    m = n * PRODS + j
                    if m >= SLOTS:
                        pn, pj = divmod(m - SLOTS, PRODS)
                        if pj == PRODS - 1:
                            pt, pc = divmod(pn, STEPS * NBANK)
                            dve.wait_ge(s_bank, full(pt, "pde", pc))
                        else:
                            dve.wait_ge(s_summed, pn * (PRODS - 1) + pj + 1)
                    dve.tensor_tensor(prod[:, m % SLOTS, :].rearrange("p (w c) -> p w c", c=C),
                                      wc(arr[coef][:, :])[:, a:b, :],
                                      h[:, a + w0:b + w0, c0:c0 + C], ALU.mult).then_inc(s_prod, 1)

            def chunk_end(t, it, q):
                n = (t * STEPS + it) * NBANK + q
                c = (it + q) % NBANK
                dst = h_pad[(it + 1) % 2]
                dve.wait_ge(s_bank, full(t, "pde", it * NBANK + q))
                dve.tensor_tensor(dst[:, c * CHUNK_W + 1:(c + 1) * CHUNK_W + 1, 1:C + 1],
                                  bank("pde", it * NBANK + q).rearrange("p (w c) -> p w c", c=C),
                                  rest[:, n % 2, :].rearrange("p (w c) -> p w c", c=C), ALU.add).then_inc(s_dve, 1)

            def iteration(t, it):
                for q in range(NBANK):
                    chunk_products(t, it, q)
                    if q:
                        chunk_end(t, it, q - 1)
                    elif it:
                        chunk_end(t, it - 1, NBANK - 1)

            def add_conv(t):
                chunk_end(t, STEPS - 1, NBANK - 1)
                dve.wait_ge(*emptied(t, "pde", STEPS * NBANK - 1))
                y = wc(arr[0][:, :])
                row = [P, W, C]
                seq(dve.tensor_tensor(y, inner(h_pad[STEPS % 2]), bn_scale[:, 2, :].unsqueeze(1).to_broadcast(row), ALU.mult))
                seq(dve.tensor_tensor(y, y, bn_shift[:, 2, :].unsqueeze(1).to_broadcast(row), ALU.add))
                seq(dve.scalar_tensor_tensor(x1[t][:, :], arr[0][:, :], 0.0, x1[t][:, :], ALU.max, ALU.add))

            def sampling(t, q):
                n, n9 = QCOLS * 2 * K2, QCOLS * K2
                z = arr[1][:, q * QCOLS * OFFS:(q + 1) * QCOLS * OFFS].rearrange("p (w o) -> p w o", o=OFFS)
                dve.wait_ge(s_bank, full(t, "offback", q))
                if t == 0 and q == 0:
                    dve.wait_ge(s_offb, 16)
                dve.tensor_tensor(z, bank("offback", q)[:, 0:QCOLS * OFFP].rearrange("p (w o) -> p w o", o=OFFP)[:, :, 0:OFFS],
                                  off_b[:, :].unsqueeze(1).to_broadcast([P, QCOLS, OFFS]), ALU.add).then_inc(s_dve, 1)
                dve.wait_ge(*emptied(t, "offback", q))

                def wo(a):
                    return a.rearrange("p (w o) -> p w o", o=2 * K2)

                def wk(a):
                    return a.rearrange("p (w k) -> p w k", k=K2)

                pos, low, above = arr[3][:, 0:n], arr[4][:, 0:n], arr[5][:, 0:n]
                seq(dve.tensor_tensor(wo(pos), z[:, :, 0:2 * K2], base_pos[:, q * QCOLS:(q + 1) * QCOLS, :], ALU.add))
                seq(dve.tensor_scalar(pos, pos, CLIP_LOW, CLIP_HIGH, ALU.max, ALU.min))
                seq(dve.tensor_copy(pos_int[:, 0:n], pos))
                seq(dve.tensor_copy(low, pos_int[:, 0:n]))
                seq(dve.tensor_tensor(above, low, pos, ALU.is_gt))
                seq(dve.tensor_tensor(low, low, above, ALU.subtract))
                entry = above[:, 0:n9]
                seq(dve.scalar_tensor_tensor(wk(entry), wo(low)[:, :, 0:K2], float(TX), wo(low)[:, :, K2:2 * K2],
                                             ALU.mult, ALU.add))
                at = t * W * K2 + q * n9
                dve.tensor_scalar(index[:, at:at + n9], entry, const[:, C_ENT + t:C_ENT + t + 1], None,
                                  ALU.add).then_inc(s_index, 1)
                seq(dve.tensor_tensor(pos, pos, low, ALU.subtract))
                dy, dx = wo(pos)[:, :, 0:K2], wo(pos)[:, :, K2:2 * K2]
                mask, bottom, top = arr[2][:, q * n9:(q + 1) * n9], arr[0][:, 0:n9], arr[0][:, n9:2 * n9]
                corner = corner_w[:, t, q * QCOLS:(q + 1) * QCOLS, :].rearrange("p w (k j) -> p w k j", j=4)
                dve.wait_ge(s_mask, QUARTERS * t + q + 1)
                dve.wait_ge(s_cleared, 16 * B)
                seq(dve.tensor_tensor(wk(bottom), wk(mask), dy, ALU.mult))
                seq(dve.tensor_tensor(top, mask, bottom, ALU.subtract))
                seq(dve.tensor_tensor(corner[:, :, :, 3], wk(bottom), dx, ALU.mult))
                seq(dve.tensor_tensor(corner[:, :, :, 2], wk(bottom), corner[:, :, :, 3], ALU.subtract))
                seq(dve.tensor_tensor(corner[:, :, :, 1], wk(top), dx, ALU.mult))
                seq(dve.tensor_tensor(corner[:, :, :, 0], wk(top), corner[:, :, :, 1], ALU.subtract))

            def stage(t, k):
                if k == 0:
                    if t == 0:
                        dve.memset(corner_w[:, 0, :, :], 0.0).then_inc(s_zeros, 1)
                    dve.wait_ge(s_x[t], 16)
                    if t:
                        dve.wait_ge(s_table, 16 * 2 * IMGS * t)
                    group_norm(2 * t, wc(x1[t][:, :]), wc(xn_flat), arr[0][:, :], s_xn)
                    if t == 0:
                        parameters()
                    sobel(t)
                elif k == 1:
                    diffusion(t)
                    dve.wait_ge(s_halo, t + 1)
                    gate_banks(t, 0)
                elif k == 2:
                    gate_banks(t, NBANK)
                    transport(t)
                elif k < N_STAGES - 1:
                    iteration(t, k - 3)
                else:
                    add_conv(t)
                    seq(dve.memset(xn_pad[:, 0, :], 0.0))
                    seq(dve.memset(xn_pad[:, W + 1, :], 0.0))
                    group_norm(2 * t + 1, wc(x1[t][:, :]), xn_pad[:, 1:W + 1, :], arr[0][:, :], s_xn2)
                    for q in range(QUARTERS):
                        sampling(t, q)

            def group(t, g):
                big = g + t * GATHER_GROUPS
                for j in range(COLS):
                    col = big * COLS + j
                    px = pixels[:, j, :, :]
                    quads = px.rearrange("p k (q c) -> p (k q) c", c=C)
                    dve.wait_ge(s_pixels[j], big * (16 * K2) + 16 * K2)
                    weights = corner_w[:, t, :, :].rearrange("p w k -> p (w k)")[:, bass.ds(g * (COLS * 4 * K2) + j * 4 * K2, 4 * K2)]
                    dve.tensor_tensor(quads, quads, weights.unsqueeze(2).to_broadcast([P, 4 * K2, C]), ALU.mult)\
                       .then_inc(s_weighted, 1)
                    dve.wait_ge(s_weighted, col + 1)
                    dve.tensor_tensor(px[:, :, 0:2 * C], px[:, :, 0:2 * C], px[:, :, 2 * C:4 * C], ALU.add)\
                       .then_inc(s_halved, 1)
                dve.wait_ge(s_out, big * COLS + COLS)
                here = x1[t][:, bass.ds(g * (COLS * C), COLS * C)]
                dve.tensor_tensor(here, out_ps, here, ALU.add).then_inc(s_x2, 1)

            dve.memset(one[:, :], 1.0).then_inc(s_part, COLS * PARTS)

            def groups_loop(t):
                with dve.Fori(0, GATHER_GROUPS, 1) as g:
                    group(t, g)

            interleave(stage, group, groups_loop)

        @block.scalar
        def _(act):
            steps = [0]

            def seq(ins):
                steps[0] += 1
                ins.then_inc(s_a, 1)
                act.wait_ge(s_a, steps[0])

            def norm(k, centred, square):
                act.wait_ge(s_centred, k + 1)
                act.activation(wc(square), centred, ACT.Square).then_inc(s_square, 1)
                act.wait_ge(s_ve, k + 1)
                act.activation(grstd[:, :], gvar[:, :], ACT.Sqrt).then_inc(s_sd, 1)

            def channel_halo(h, a, b):
                act.activation(h[:, a + 1:b + 1, 0:1], h[:, a + 1:b + 1, C:C + 1], ACT.Copy)
                return act.activation(h[:, a + 1:b + 1, C + 1:C + 2], h[:, a + 1:b + 1, 1:2], ACT.Copy)

            def column_halo(h, right):
                to, of = (W + 1, 1) if right else (0, W)
                return act.activation(h[:, to, 1:C + 1], h[:, of, 1:C + 1], ACT.Copy)

            def turn_banks(t, what):
                def rows(a):
                    return a.rearrange("p (w h) -> p w h", h=H)

                for q in range(NBANK):
                    act.wait_ge(s_bank, full(t, what, q))
                    src = rows(bank(what, q))
                    above, same, below = (rows(a[:, q * BANK:(q + 1) * BANK]) for a in xT)
                    act.activation(same, src, ACT.Copy)
                    act.activation(above[:, :, 1:H], src[:, :, 0:H - 1], ACT.Copy)
                    act.activation(above[:, :, 0], eye[:, 0:BANK // H], ACT.Copy, scale=0.0)
                    act.activation(below[:, :, H - 1], eye[:, 0:BANK // H], ACT.Copy, scale=0.0)
                    act.activation(below[:, :, 0:H - 1], src[:, :, 1:H], ACT.Copy).then_inc(s_act, 1)

            def masks(t, q):
                act.wait_ge(*emptied(t, "offback", q))
                z = arr[1][:, q * QCOLS * OFFS:(q + 1) * QCOLS * OFFS].rearrange("p (w o) -> p w o", o=OFFS)
                act.activation(arr[2][:, q * QCOLS * K2:(q + 1) * QCOLS * K2].rearrange("p (w k) -> p w k", k=K2),
                               z[:, :, 2 * K2:OFFS], ACT.Sigmoid).then_inc(s_mask, 1)

            def chunk_halo(t, it, q):
                c = (it + q) % NBANK
                h = h_pad[(it + 1) % 2]
                act.wait_ge(*emptied(t, "pde", it * NBANK + q))
                if c == 0:
                    column_halo(h, True)
                if c == NBANK - 1:
                    column_halo(h, False)
                channel_halo(h, c * CHUNK_W, (c + 1) * CHUNK_W).then_inc(s_hhalo, 1)

            def stage(t, k):
                if k == 0:
                    norm(2 * t, wc(xn_flat), arr[0][:, :])
                    if t == 0:
                        act.wait_ge(s_bn_ve, 1)
                        act.activation(bn_scale[:, :, :], bn[:, 3, :, :], ACT.Sqrt).then_inc(s_bn_sd, 1)
                    turn_banks(t, "turn")
                    for i, what in enumerate(("diff", "smooth")):
                        act.wait_ge(s_bank, full(t, what, NBANK - 1))
                        act.activation(arr[i][:, :], flat(acc[:, :, :]), ACT.Copy).then_inc(s_act, NBANK)
                    for i in range(2):
                        act.wait_ge(s_grad, 2 * t + i + 1)
                        act.activation(arr[2 + i][:, :], arr[2 + i][:, :], ACT.Square, scale=0.5).then_inc(s_grad2, 1)
                    seq(act.activation(inner(h_pad[0]), wc(xn_flat), ACT.Copy))
                    column_halo(h_pad[0], True)
                    column_halo(h_pad[0], False)
                    channel_halo(h_pad[0], 0, W).then_inc(s_halo, 1)
                elif k == 1:
                    act.wait_ge(s_den, t + 1)
                    seq(act.activation(arr[1][:, :], arr[0][:, :], ACT.Ln))
                    act.activation(arr[1][:, :], arr[1][:, :], ACT.Exp, scale=-1.0).then_inc(s_seed, 1)
                    act.wait_ge(s_pq, t + 1)
                    act.activation(arr[4][:, :], arr[0][:, :], ACT.Identity, bias=one[:, 0:1], scale=-2.0).then_inc(s_c0, 1)
                elif k == 2:
                    act.wait_ge(*emptied(t, "conv", 2 * NBANK - 1))
                    seq(act.activation(inner(gx_pad), inner(gx_pad), ACT.Relu))
                    column_halo(gx_pad, True)
                    column_halo(gx_pad, False).then_inc(s_gates, 1)
                    seq(act.activation(inner(h_pad[1]), inner(h_pad[1]), ACT.Relu))
                    channel_halo(h_pad[1], 0, W).then_inc(s_gates, 1)
                elif k < N_STAGES - 1:
                    it = k - 3
                    if it:
                        chunk_halo(t, it - 1, NBANK - 1)
                    if it < STEPS - 1:
                        for q in range(NBANK - 1):
                            chunk_halo(t, it, q)
                else:
                    norm(2 * t + 1, xn_pad[:, 1:W + 1, :], arr[0][:, :])
                    turn_banks(t, "turn2")
                    for q in range(QUARTERS):
                        act.wait_ge(s_bank, full(t, "off", q))
                        act.activation(arr[6][0:2 * OFFP, q * BANK:(q + 1) * BANK], bank("off", q)[0:2 * OFFP, :],
                                       ACT.Copy).then_inc(s_act, 1)
                        if q:
                            masks(t, q - 1)
                    masks(t, QUARTERS - 1)

            def group(t, g):
                big = g + t * GATHER_GROUPS
                for j in range(COLS):
                    col = big * COLS + j
                    if not (isinstance(g, int) and big * COLS + j < 2):
                        act.wait_ge(s_out, col - 1)
                    for r in range(PARTS):
                        act.wait_ge(s_part, col * PARTS + (r + 1 + COLS * PARTS))
                        act.activation(sampled_T[:, j % 2, r * PART * P:(r + 1) * PART * P],
                                       turned[:, r, 0:PART * P], ACT.Copy).then_inc(s_sT, 1)

            def groups_loop(t):
                with act.Fori(0, GATHER_GROUPS, 1) as g:
                    group(t, g)

            interleave(stage, group, groups_loop)

        @block.tensor
        def _(pe):
            def group_sums(k):
                pe.wait_ge(s_rsum, k + 1)
                if k == 0:
                    pe.wait_ge(s_const, 16)
                pe.matmul(stat_ps, ones_block, rsum[:, :], start=True, stop=True).then_inc(s_stat, 1)

            def turn(t, what, src):
                for q in range(NBANK):
                    wait_bank_empty(pe, t, what, q)
                    for i in range(PAIRS_BANK):
                        pair = q * PAIRS_BANK + i
                        ins = pe.transpose(bank(what, q)[:, i * P:(i + 1) * P], src[:, pair * P:(pair + 1) * P], eye)
                    ins.then_inc(s_bank, 1)

            def turned_pair(dh, pair):
                return xT[dh][:, pair * P:(pair + 1) * P]

            def depthwise(t):
                per_bank = BANK // (4 * C)
                for q in range(2 * NBANK):
                    wait_bank_empty(pe, t, "conv", q)
                    for i in range(per_bank):
                        pair = q * per_bank + i
                        dst = bank("conv", q)[:, i * 4 * C:(i + 1) * 4 * C]
                        for dh in range(3):
                            w3 = conv_w[:, dh, :, :].rearrange("p a b -> p (a b)")
                            ins = pe.matmul(dst, turned_pair(dh, pair), w3[:, 0:4 * C], start=dh == 0, stop=False)
                            if pair > 0:
                                ins = pe.matmul(dst[:, 0:2 * C], turned_pair(dh, pair - 1), w3[:, 4 * C:6 * C],
                                                start=False, stop=dh == 2 and pair == PAIRS - 1)
                            if pair < PAIRS - 1:
                                ins = pe.matmul(dst[:, 2 * C:4 * C], turned_pair(dh, pair + 1), w3[:, 6 * C:8 * C],
                                                start=False, stop=dh == 2)
                    ins.then_inc(s_bank, 1)

            def offsets(t, q):
                wait_bank_empty(pe, t, "off", q)
                dst = bank("off", q)[0:2 * OFFP, :]
                a, b = q * BANK, (q + 1) * BANK
                for dh in range(3):
                    pe.matmul(dst, off_w[:, dh, 0, :], xT[dh][:, a:b], start=dh == 0, stop=False)
                    skip = P if q == 0 else 0
                    pe.matmul(dst[:, skip:BANK], off_w[:, dh, 1, :], xT[dh][:, a - P + skip:b - P],
                              start=False, stop=False)
                    skip = P if q == QUARTERS - 1 else 0
                    ins = pe.matmul(dst[:, 0:BANK - skip], off_w[:, dh, 2, :], xT[dh][:, a + P:b + P - skip],
                                    start=False, stop=dh == 2)
                ins.then_inc(s_bank, 1)

            def offsets_back(t, q):
                pe.wait_ge(*emptied(t, "off", q))
                wait_bank_empty(pe, t, "offback", q)
                for i in range(PAIRS_BANK):
                    ins = pe.transpose(bank("offback", q)[:, i * 2 * OFFP:(i + 1) * 2 * OFFP],
                                       arr[6][0:2 * OFFP, q * BANK + i * P:q * BANK + (i + 1) * P],
                                       eye[0:2 * OFFP, 0:2 * OFFP])
                ins.then_inc(s_bank, 1)

            def stage(t, k):
                if k == 0:
                    group_sums(4 * t)
                    group_sums(4 * t + 1)
                    pe.wait_ge(s_xn, t + 1)
                    turn(t, "turn", xn_flat)
                    for what, over_rows in (("diff", diff_h), ("smooth", smooth_h)):
                        for q in range(NBANK):
                            wait_bank_empty(pe, t, what, q)
                            pe.matmul(bank(what, q), over_rows, xn_flat[:, q * BANK:(q + 1) * BANK],
                                      start=True, stop=True).then_inc(s_bank, 1)
                elif k == 1:
                    if t == 0:
                        pe.wait_ge(s_conv_w, 1)
                    pe.wait_ge(*emptied(t, "turn", NBANK - 1))
                    depthwise(t)
                elif k == 2:
                    pe.wait_ge(s_gates, 2 * t + 2)
                    for q in range(NBANK):
                        wait_bank_empty(pe, t, "own", q)
                        a, b = q * CHUNK_W, (q + 1) * CHUNK_W
                        pe.matmul(bank("own", q), eye, gx_pad[:, a + 2:b + 2, 1:C + 1], start=True, stop=False)
                        pe.matmul(bank("own", q), minus_eye, gx_pad[:, a:b, 1:C + 1], start=False, stop=False)
                        pe.matmul(bank("own", q), eye, h_pad[1][:, a + 1:b + 1, 2:C + 2], start=False, stop=False)
                        pe.matmul(bank("own", q), minus_eye, h_pad[1][:, a + 1:b + 1, 0:C], start=False, stop=True)\
                          .then_inc(s_bank, 1)
                elif k < N_STAGES - 1:
                    it = k - 3
                    for q in range(NBANK):
                        n = (t * STEPS + it) * NBANK + q
                        wait_bank_empty(pe, t, "pde", it * NBANK + q)
                        for j in range(PRODS):
                            m = n * PRODS + j
                            pe.wait_ge(s_prod, m + 1)
                            pe.matmul(bank("pde", it * NBANK + q), eye, prod[:, m % SLOTS, :],
                                      start=j == 0, stop=j == PRODS - 1)\
                              .then_inc(s_bank if j == PRODS - 1 else s_summed, 1)
                else:
                    group_sums(4 * t + 2)
                    group_sums(4 * t + 3)
                    pe.wait_ge(s_xn2, t + 1)
                    turn(t, "turn2", scratch[:, C:C + WC])
                    pe.wait_ge(*emptied(t, "turn2", NBANK - 1))
                    if t == 0:
                        pe.wait_ge(s_offw, 16)
                    for what, q, _ in PLAN[AT["off", 0]:]:
                        (offsets if what == "off" else offsets_back)(t, q)

            def group(t, g):
                big = g + t * GATHER_GROUPS
                first = isinstance(g, int) and t == 0 and g == 0
                if first:
                    pe.wait_ge(s_filt, 32)
                for j in range(COLS):
                    col = big * COLS + j
                    pe.wait_ge(s_halved, col + 1)
                    for r in range(PARTS):
                        m = col * PARTS + r
                        if not (first and j * PARTS + r < PART_SLOTS):
                            pe.wait_ge(s_sT, m - (PART_SLOTS - 1))
                        for i in range(PART):
                            ins = pe.transpose(turned[:, r, i * P:(i + 1) * P],
                                               pixels[:, j, r * PART + i, 0:2 * C], eye)
                        ins.then_inc(s_part, 1)
                    pe.wait_ge(s_sT, (col + 1) * PARTS)
                    if j == 0 and not first:
                        pe.wait_ge(s_x2, big)
                    for k in range(K2):
                        ins = pe.matmul(out_ps[:, j * C:(j + 1) * C], sampled_T[:, j % 2, k * P:(k + 1) * P],
                                        filt[:, k, :], start=k == 0, stop=k == K2 - 1)
                    ins.then_inc(s_out, 1)

            def groups_loop(t):
                with pe.Fori(0, GATHER_GROUPS, 1) as g:
                    group(t, g)

            interleave(stage, group, groups_loop)


def constants():
    row = np.arange(P)
    h = row % H
    image = row // H
    c = np.zeros((P, C_ALL), np.float32)
    c[:, C_EYE:C_EYE + P] = np.eye(P)
    c[:, C_NEG:C_NEG + P] = -np.eye(P)
    same = image[:, None] == image[None, :]
    c[:, C_ONES:C_ONES + P] = same
    for m in range(P):
        first = m - h[m]
        below = h[m] + 1 if h[m] < H - 1 else H - 2
        above = h[m] - 1 if h[m] > 0 else 1
        c[first + below, C_DIFF + m] += 1
        c[first + above, C_DIFF + m] -= 1
        c[first + below, C_SMOOTH + m] += 1
        c[m, C_SMOOTH + m] += 2
        c[first + above, C_SMOOTH + m] += 1
    c[:, C_MASK:C_MASK + C] = (row % C)[:, None] == np.arange(C)[None, :]
    k = np.arange(K2)
    base = np.zeros((P, W, 2 * K2), np.float32)
    base[:, :, 0:K2] = h[:, None, None] - 1 + (k // 3)[None, None, :]
    base[:, :, K2:] = np.arange(W)[None, :, None] - 1 + (k % 3)[None, None, :]
    c[:, C_BASE:C_ENT] = base.reshape(P, -1)
    for t in range(TILES):
        c[:, C_ENT + t] = (t * IMGS + image) * TY * TX + LO * TX + LO
    return c


def by_parity(w):
    none = np.zeros_like(w[:, 0])
    even = np.stack([w[:, 1], w[:, 0], none, w[:, 2]], 0)
    odd = np.stack([w[:, 2], w[:, 1], w[:, 0], none], 0)
    both = np.stack([even, odd], 0)
    return both.transpose(0, 3, 2, 1, 4).reshape(P, 3, 4, -1)


def stationary(blocks):
    blocks = np.pad(blocks, ((0, 0), (0, 0), (0, 0), (0, OFFP - OFFS)))
    none = np.zeros_like(blocks[:, :, 0])
    parts = [blocks[:, :, 0], blocks[:, :, 1], blocks[:, :, 2], none, none, blocks[:, :, 3]]
    return np.ascontiguousarray(np.stack(parts, 2).reshape(P, -1))


def kernel(x, L0_conv_wg, L0_conv_wg1, L0_conv_g_gamma, L0_conv_g_beta, L0_conv_g_mean, L0_conv_g_var,
           L0_conv_g1_gamma, L0_conv_g1_beta, L0_conv_g1_mean, L0_conv_g1_var, L0_conv_out_gamma,
           L0_conv_out_beta, L0_conv_out_mean, L0_conv_out_var, L1_conv_w_offset, L1_conv_b_offset,
           L1_conv_filt):
    import concourse.bacc as bacc
    from concourse.bass_utils import run_bass_kernel_spmd

    bn = np.stack([L0_conv_g_gamma, L0_conv_g1_gamma, L0_conv_out_gamma,
                   L0_conv_g_beta, L0_conv_g1_beta, L0_conv_out_beta,
                   L0_conv_g_mean, L0_conv_g1_mean, L0_conv_out_mean,
                   L0_conv_g_var, L0_conv_g1_var, L0_conv_out_var], 0)
    arrays = {
        "x_in": np.ascontiguousarray(np.asarray(x).reshape(TILES * P, WC)),
        "taps_in": np.ascontiguousarray(by_parity(np.stack([np.asarray(L0_conv_wg), np.asarray(L0_conv_wg1)], -1))
                                        .reshape(P, -1)),
        "offw_in": stationary(by_parity(np.asarray(L1_conv_w_offset))),
        "filt_in": np.ascontiguousarray(np.asarray(L1_conv_filt).transpose(1, 2, 3, 0).reshape(C, K2 * C)),
        "bn_in": np.ascontiguousarray(bn.reshape(1, 12 * C)),
        "offb_in": np.ascontiguousarray(np.asarray(L1_conv_b_offset).reshape(1, OFFS)),
        "const_in": constants(),
    }
    nc = bacc.Bacc("TRN2", target_bir_lowering=False, num_devices=1)
    args = [nc.dram_tensor(n, a.shape, mybir.dt.from_np(a.dtype), kind="ExternalInput").ap()
            for n, a in arrays.items()]
    out = nc.dram_tensor("out_dram", [TILES * P, WC], mybir.dt.float32, kind="ExternalOutput").ap()
    build_program(nc, *args, out)
    r = run_bass_kernel_spmd(nc, [arrays], core_ids=[0])
    return r.results[0]["out_dram"].reshape(B, H, W, C)
```

```python
import concourse.bass as bass
from concourse import mybir
from contextlib import ExitStack
import numpy as np

B, H, W, C = 8, 32, 32, 64
P = 128
IMGS = P // H
TILES = B // IMGS
WC = W * C
GROUP_SIZE = 2
GROUPS = C // GROUP_SIZE
K2 = 9
OFFS = 3 * K2
DT, BN_EPS, GN_EPS = 0.2, 0.001, 1e-05
STEPS = 5
LO = 2
TY = TX = H + LO + 1
ENTRY = 4 * C
ENTRIES = B * TY * TX
CLIP_LOW, CLIP_HIGH = -float(LO), H + 0.5
BANK = 512
NBANK = WC // BANK
CHUNK_W = BANK // C
PAIRS = W // 2
PAIRS_BANK = PAIRS // NBANK
QUARTERS = NBANK
QCOLS = W // QUARTERS
OFFP = 32
COLS = 4
GATHER_GROUPS = W // COLS
PARTS = 3
PART = K2 // PARTS
PART_SLOTS = 2
NORM_SUMS = 4
PRODS = 5
SLOTS = 6
C_EYE, C_ONES, C_DIFF, C_SMOOTH, C_MASK, C_NEG, C_BASE = 0, 128, 256, 384, 512, 576, 704
C_ENT = C_BASE + W * 2 * K2
C_ALL = C_ENT + TILES
PIECES = (["sum1", "centre1", "square1", "deviation1", "scale1", "turn", "rows", "sobel", "denominator"]
          + [f"conv {i}" for i in range(4)] + [f"gates {i}" for i in range(4)] + ["coefficients", "forcing",
          "transport x", "transport y"] + [f"pde {i}" for i in range(STEPS * NBANK)] + ["add", "sum2", "centre2",
          "square2", "deviation2", "scale2", "turn2"] + [f"{s} {q}" for q in range(QUARTERS)
                                                         for s in ("offsets", "sampling")])
MAKES = {"sum1": [("sum", 0, "dve")], "square1": [("sum", 1, "dve")], "sum2": [("sum", 2, "dve")],
         "square2": [("sum", 3, "dve")], "turn": [("turn", q, "act") for q in range(NBANK)],
         "rows": [("rows", q, "act") for q in range(2 * NBANK)],
         "transport x": [("own", q, "dve") for q in range(NBANK)],
         "turn2": [("turn2", q, "act") for q in range(NBANK)]}
MAKES.update({f"conv {i}": [("conv", q, "dve") for q in (2 * i, 2 * i + 1)] for i in range(4)})
MAKES.update({f"pde {q}": [("pde", q, "dve")] for q in range(STEPS * NBANK)})
MAKES.update({f"offsets {q}": [("off", q, "act"), ("offback", q, "dve")] for q in range(QUARTERS)})
COL = "column"
FIRST = ["sum1", "centre1", "square1", "deviation1", "scale1", "turn", "rows", "conv 0", "sobel", "denominator",
         "gates 0", "conv 1", "coefficients", "gates 1", "conv 2", "forcing", "gates 2", "conv 3", "gates 3",
         "transport x", "transport y"] + [f"pde {i}" for i in range(STEPS * NBANK)] + \
        ["add", "sum2", "centre2", "square2", "deviation2", "scale2", "turn2", "offsets 0"]
ORDER = ([(0, p) for p in FIRST]
         + [(0, "offsets 1"), (0, "sampling 0"), (1, "sum1"), (0, "offsets 2"), (0, "sampling 1"),
            (1, "centre1"), (0, "offsets 3"), (0, "sampling 2"), (1, "square1"), (0, "sampling 3")]
         + [(1, p) for p in
            ["deviation1", COL, "scale1", "turn", COL, "rows", COL, "conv 0", "sobel", COL, "denominator", COL,
             "conv 1", "gates 0", "gates 1", COL, "coefficients", "conv 2", "forcing", COL, "gates 2",
             "conv 3", COL, "gates 3", "transport x", COL, "transport y", COL]
            + [p for i in range(STEPS * NBANK) for p in [f"pde {i}"] + [COL] * (i % 3 != 2 and i < 18)]
            + ["add", COL, "sum2", "centre2", "square2", COL, "deviation2", "scale2", COL, "turn2", "offsets 0",
               COL, "sampling 0", "offsets 1", COL, "sampling 1", "offsets 2", COL, "sampling 2", COL, "offsets 3",
               COL, "sampling 3"]])
N_COLS = [p for t, p in ORDER].count(COL)
assert N_COLS <= W, N_COLS
ORDER += [(1, COL)] * (W - N_COLS)
PLAN = [(t,) + made for t, piece in ORDER for made in MAKES.get(piece, [])]
AT = {made[:3]: n for n, made in enumerate(PLAN)}


def build_program(nc, x_in, taps_in, offw_in, filt_in, bn_in, offb_in, const_in, out_dram):
    f32, i32, u32 = mybir.dt.float32, mybir.dt.int32, mybir.dt.uint32
    ALU, ACT, AX = mybir.AluOpType, mybir.ActivationFunctionType, mybir.AxisListType
    table = nc.dram_tensor("table", [ENTRIES, ENTRY], f32, kind="Internal").ap()
    table_y = table.rearrange("(b y x) e -> b y x e", b=B, y=TY)

    with ExitStack() as ctx:
        def sb(name, shape, dt=f32):
            return ctx.enter_context(nc.sbuf_tensor(name, shape, dt))

        def psum(name, shape):
            return ctx.enter_context(nc.psum_tensor(name, shape, f32))

        def sem(name):
            return ctx.enter_context(nc.semaphore(name))

        const = sb("const", [P, C_ALL])
        eye = const[:, C_EYE:C_EYE + P]
        ones_block = const[:, C_ONES:C_ONES + P]
        diff_h = const[:, C_DIFF:C_DIFF + P]
        smooth_h = const[:, C_SMOOTH:C_SMOOTH + P]
        minus_eye = const[:, C_NEG:C_NEG + P]
        same_c = const[:, C_MASK:C_MASK + C]
        base_pos = const[:, C_BASE:C_ENT].rearrange("p (w o) -> p w o", o=2 * K2)
        taps = sb("taps", [P, 3, 4, 2])
        conv_w = sb("conv_w", [P, 3, 4, 2 * C])
        off_w = sb("off_w", [P, 3, 3, 2 * OFFP])
        filt = sb("filt", [P, K2, C])
        off_b = sb("off_b", [P, OFFS])
        bn = sb("bn", [P, 4, 3, C])
        bn_scale = sb("bn_scale", [P, 3, C])
        bn_shift = sb("bn_shift", [P, 3, C])
        x1 = [sb(f"x1_{t}", [P, WC]) for t in range(TILES)]
        h_pad = [sb(f"h_pad{i}", [P, W + 2, C + 2]) for i in range(2)]
        scratch = sb("scratch", [P, (W + 2) * (C + 2)])
        xn_flat = scratch[:, 0:WC]
        gx_pad = scratch[:, :].rearrange("p (w c) -> p w c", c=C + 2)
        xn_pad = scratch[:, 0:(W + 2) * C].rearrange("p (w c) -> p w c", c=C)
        xT_mid = sb("xT_mid", [P, WC])
        shared = sb("shared", [P, 2 * WC])
        xT = (shared[:, 0:WC], xT_mid[:, :], shared[:, WC:2 * WC])
        arr = [sb(f"arr{i}", [P, WC]) for i in range(7)]
        prod = shared[:, 0:SLOTS * BANK].rearrange("p (s n) -> p s n", n=BANK)
        rest = shared[:, SLOTS * BANK:(SLOTS + 2) * BANK].rearrange("p (s n) -> p s n", n=BANK)
        rsum = sb("rsum", [P, C])
        gmean = sb("gmean", [P, GROUPS])
        gvar = sb("gvar", [P, GROUPS])
        grstd = sb("grstd", [P, GROUPS])
        gtmp = sb("gtmp", [P, GROUPS])
        one = sb("one", [P, 1])
        pos_int = sb("pos_int", [P, W * 2 * K2], i32)
        corner_w = sb("corner_w", [P, TILES, W, K2 * 4])
        index = sb("index", [P, TILES * W * K2], u32)
        index_now = sb("index_now", [P, 2, COLS, K2], u32)
        pixels = sb("pixels", [P, COLS, K2, ENTRY])
        sampled_T = sb("sampled_T", [P, 2, K2 * P])
        acc = psum("acc", [P, NBANK, BANK])
        side = psum("side", [P, NBANK, BANK])
        turned = side[:, 0:PART_SLOTS, :]
        out_ps = [side[:, 2, 0:COLS * C], side[:, 3, 0:COLS * C]]

        s_const, s_taps, s_offw, s_filt, s_bn, s_offb = (
            sem(n) for n in ("const_in", "taps_in", "offw_in", "filt_in", "bn_in", "offb_in"))
        s_x = [sem(f"x_in{t}") for t in range(TILES)]
        s_zeros = sem("zeros_ready")
        s_cleared = sem("table_cleared")
        s_table = sem("table_written")
        s_conv_w = sem("conv_w_ready")
        s_bn_ve = sem("bn_var_eps_ready")
        s_bn_sd = sem("bn_sd_ready")
        s_rsum = sem("row_sums_ready")
        s_centred = sem("centred_ready")
        s_square = sem("squares_ready")
        s_ve = sem("var_eps_ready")
        s_sd = sem("sd_ready")
        s_xn = sem("xn_ready")
        s_halo = sem("xn_halo_ready")
        s_bank = sem("bank_full")
        s_act = sem("bank_emptied_by_act")
        s_dve = sem("bank_emptied_by_dve")
        s_sobel = sem("gradient_ready")
        s_grad2 = sem("squared_gradients_ready")
        s_den = sem("denominator_ready")
        s_seed = sem("reciprocal_seed_ready")
        s_pq = sem("p_plus_q_ready")
        s_c0 = sem("c0_ready")
        s_gates = sem("gates_ready")
        s_prod = sem("product_ready")
        s_summed = sem("product_summed")
        s_rest = sem("rest_ready")
        s_hhalo = sem("h_halo_ready")
        s_xn2 = sem("xn2_ready")
        s_mask = sem("mask_ready")
        s_index = sem("index_ready")
        s_copied = sem("indices_copied")
        s_begun = sem("column_begun")
        s_pixels = [sem(f"pixels_in{j}") for j in range(COLS)]
        s_halved = sem("halved_ready")
        s_part = sem("part_turned")
        s_sT = sem("sampled_T_ready")
        s_weighted = sem("weighted")
        s_out = sem("column_filtered")
        s_x2 = sem("group_added")
        s_store = sem("stored")
        s_v = sem("vector_step")
        s_a = sem("scalar_step")

        block = ctx.enter_context(nc.Block())

        def flat(a):
            return a.rearrange("p w c -> p (w c)")

        def wc(a):
            return a.rearrange("p (w c) -> p w c", c=C)

        def inner(a):
            return a[:, 1:W + 1, 1:C + 1]

        def emptied(t, what, q):
            n = AT[t, what, q]
            who = PLAN[n][3]
            return {"act": s_act, "dve": s_dve}[who], [p[3] for p in PLAN[:n + 1]].count(who)

        def full(t, what, q):
            return AT[t, what, q] + 1

        def bank(t, what, q):
            return acc[:, AT[t, what, q] % NBANK, :]

        def wait_bank_empty(pe, t, what, q):
            n = AT[t, what, q] - NBANK
            if n >= 0:
                pe.wait_ge(*emptied(*PLAN[n][:3]))

        def in_order(eng, piece, column):
            done = 0
            for t, name in ORDER:
                if name == COL:
                    column(0, done // COLS, done % COLS)
                    done += 1
                else:
                    piece(t, *name.split())
            for j in range(COLS):
                column(1, 0, j)
            with eng.Fori(0, GATHER_GROUPS // 2 - 1, 1) as i:
                for odd in (1, 0):
                    for j in range(COLS):
                        column(1, i * 2 + (2 - odd), j, odd)
            for j in range(COLS):
                column(1, GATHER_GROUPS - 1, j)

        def parity(g, odd):
            return g % 2 if odd is None else odd

        @block.sync
        def _(sp):
            sp.dma_start(x1[0][:, :], x_in[0:P, :]).then_inc(s_x[0], 16)
            sp.dma_start(const[:, :], const_in).then_inc(s_const, 16)
            sp.dma_start(bn[:, :, :, :].rearrange("p a b c -> p (a b c)"),
                         bn_in.to_broadcast([P, 12 * C])).then_inc(s_bn, 16)
            sp.dma_start(taps[:, :, :, :].rearrange("p a b c -> p (a b c)"), taps_in).then_inc(s_taps, 16)
            sp.dma_start(off_w[:, :, :, :].rearrange("p a b c -> p (a b c)"), offw_in).then_inc(s_offw, 16)
            for half in range(2):
                sp.dma_start(filt[half * C:(half + 1) * C, :, :].rearrange("p k f -> p (k f)"), filt_in)\
                  .then_inc(s_filt, 16)
            sp.dma_start(off_b[:, :], offb_in.to_broadcast([P, OFFS])).then_inc(s_offb, 16)
            sp.dma_start(x1[1][:, :], x_in[P:2 * P, :]).then_inc(s_x[1], 16)
            sp.wait_ge(s_zeros, 1)
            for b in range(B):
                sp.dma_start(table[b * TY * TX:(b + 1) * TY * TX, :].rearrange("(y x) e -> y x e", y=TY),
                             corner_w[0:TY, :, :, :].rearrange("p t w k -> p (t w k)")[:, 0:ENTRY]
                             .unsqueeze(1).to_broadcast([TY, TX, ENTRY])).then_inc(s_cleared, 16)
            sp.wait_ge(s_cleared, 16 * B)
            for t in range(TILES):
                sp.wait_ge(s_xn2, t + 1)
                for i in range(IMGS):
                    rows = scratch[i * H:(i + 1) * H, 0:(W + 1) * C].rearrange("p (w c) -> p w c", c=C)
                    pairs = bass.AP(tensor=rows.tensor, offset=rows.offset,
                                    ap=[list(rows.ap[0]), [C, W + 1], [1, 2 * C]])
                    for half in range(2):
                        sp.dma_start(table_y[t * IMGS + i, LO - half:LO - half + H, 1:W + 2,
                                             half * 2 * C:(half + 1) * 2 * C], pairs).then_inc(s_table, 16)
            for t in range(TILES):
                with sp.Fori(0, GATHER_GROUPS, 1) as g:
                    sp.wait_ge(s_x2, g + (t * GATHER_GROUPS + 1))
                    sp.dma_start(out_dram[t * P:(t + 1) * P, bass.ds(g * (COLS * C), COLS * C)],
                                 x1[t][:, bass.ds(g * (COLS * C), COLS * C)]).then_inc(s_store, 16)
            sp.wait_ge(s_store, 16 * TILES * GATHER_GROUPS)

        @block.gpsimd
        def _(pool):
            for t in range(TILES):
                pool.wait_ge(s_table, 16 * 2 * IMGS * (t + 1))
                with pool.Fori(0, QUARTERS, 1) as i:
                    pool.wait_ge(s_index, i + (t * QUARTERS + 1))
                    for half in range(2):
                        first = i * 2 + (t * GATHER_GROUPS + half)
                        pool.tensor_copy(index_now[:, half, :, :].rearrange("p j k -> p (j k)"),
                                         index[:, bass.ds(first * (COLS * K2), COLS * K2)]).then_inc(s_copied, 1)
                        pool.wait_ge(s_copied, first + 1)
                        for j in range(COLS):
                            pool.wait_ge(s_part, first * (COLS * PARTS) + (j + 1) * PARTS)
                            pool.sem_inc(s_begun, 1)
                            for k in range(K2):
                                pool.indirect_dma_start(
                                    out=pixels[:, j, k, :], out_offset=None, in_=table,
                                    in_offset=bass.IndirectOffsetOnAxis(ap=index_now[:, half, j, k:k + 1], axis=0),
                                ).then_inc(s_pixels[j], 16)


        @block.vector
        def _(dve):
            steps = [0]

            def seq(ins):
                steps[0] += 1
                ins.then_inc(s_v, 1)
                dve.wait_ge(s_v, steps[0])

            def per_group(a):
                return a[:, :].unsqueeze(1).unsqueeze(3).to_broadcast([P, W, GROUPS, GROUP_SIZE])

            def grouped(a):
                return a.rearrange("p w (g j) -> p w g j", j=GROUP_SIZE)

            def rsqrt_refined(root, v, tmp):
                seq(dve.reciprocal(root, root))
                seq(dve.tensor_tensor(tmp, root, root, ALU.mult))
                seq(dve.tensor_tensor(tmp, tmp, v, ALU.mult))
                seq(dve.tensor_scalar(tmp, tmp, -0.5, 1.5, ALU.mult, ALU.add))
                seq(dve.tensor_tensor(root, root, tmp, ALU.mult))

            def norm_mean(t, k, src, dst):
                dve.wait_ge(s_bank, full(t, "sum", k))
                dve.tensor_reduce(gmean[:, :], bank(t, "sum", k)[:, 0:C].rearrange("p (g j) -> p g j", j=GROUP_SIZE),
                                  AX.X, ALU.add).then_inc(s_dve, 1)
                dve.wait_ge(*emptied(t, "sum", k))
                seq(dve.tensor_scalar(gmean[:, :], gmean[:, :], 1.0 / (H * W * GROUP_SIZE), None, ALU.mult))
                dve.tensor_tensor(grouped(dst), grouped(src), per_group(gmean), ALU.subtract).then_inc(s_centred, 1)

            def norm_variance(t, k):
                dve.wait_ge(s_bank, full(t, "sum", k))
                dve.tensor_reduce(gvar[:, :], bank(t, "sum", k)[:, 0:C].rearrange("p (g j) -> p g j", j=GROUP_SIZE),
                                  AX.X, ALU.add).then_inc(s_dve, 1)
                dve.wait_ge(*emptied(t, "sum", k))
                dve.tensor_scalar(gvar[:, :], gvar[:, :], 1.0 / (H * W * GROUP_SIZE), GN_EPS, ALU.mult, ALU.add)\
                   .then_inc(s_ve, 1)

            def norm_scale(n, dst, ready):
                dve.wait_ge(s_sd, n + 1)
                rsqrt_refined(grstd[:, :], gvar[:, :], gtmp[:, :])
                dve.tensor_tensor(grouped(dst), grouped(dst), per_group(grstd), ALU.mult).then_inc(ready, 1)

            def row_sums(a):
                dve.tensor_reduce(rsum[:, :], a.rearrange("p w c -> p c w"), AX.X, ALU.add).then_inc(s_rsum, 1)

            def parameters():
                dve.wait_ge(s_bn, 16)
                gamma, beta, mean, var = (bn[:, i, :, :] for i in range(4))
                dve.tensor_scalar(var, var, BN_EPS, None, ALU.add).then_inc(s_bn_ve, 1)
                dve.wait_ge(s_bn_sd, 1)
                rsqrt_refined(bn_scale[:, :, :], var, bn_shift[:, :, :])
                seq(dve.tensor_tensor(bn_scale[:, :, :], bn_scale[:, :, :], gamma, ALU.mult))
                seq(dve.tensor_tensor(bn_shift[:, :, :], bn_scale[:, :, :], mean, ALU.mult))
                seq(dve.tensor_tensor(bn_shift[:, :, :], beta, bn_shift[:, :, :], ALU.subtract))
                seq(dve.tensor_scalar(bn_scale[:, 0:2, :], bn_scale[:, 0:2, :], DT, None, ALU.mult))
                seq(dve.tensor_scalar(bn_shift[:, 0:2, :], bn_shift[:, 0:2, :], DT, None, ALU.mult))
                dve.wait_ge(s_const, 16)
                dve.wait_ge(s_taps, 16)
                cells = conv_w[:, :, :, :].rearrange("p a b (g c) -> p (a b g) c", c=C)
                seq(dve.tensor_tensor(cells, same_c.unsqueeze(1).to_broadcast([P, 24, C]),
                                      taps[:, :, :, :].rearrange("p a b g -> p (a b g)").unsqueeze(2)
                                      .to_broadcast([P, 24, C]), ALU.mult))
                rows = conv_w[:, :, :, :].rearrange("p a b c -> p (a b) c")
                dve.tensor_tensor(rows, rows, bn_scale[:, 0:2, :].rearrange("p g c -> p (g c)").unsqueeze(1)
                                  .to_broadcast([P, 12, 2 * C]), ALU.mult).then_inc(s_conv_w, 1)

            def sobel(t):
                across, along = wc(arr[0][:, :]), wc(arr[1][:, :])
                gy, gx = wc(arr[2][:, :]), wc(arr[3][:, :])
                dve.wait_ge(*emptied(t, "rows", NBANK - 1))
                seq(dve.tensor_tensor(gy[:, 1:W - 1, :], across[:, 0:W - 2, :], across[:, 2:W, :], ALU.add))
                seq(dve.tensor_scalar(gy[:, 0, :], across[:, 1, :], 2.0, None, ALU.mult))
                seq(dve.tensor_scalar(gy[:, W - 1, :], across[:, W - 2, :], 2.0, None, ALU.mult))
                dve.scalar_tensor_tensor(gy, across, 2.0, gy, ALU.mult, ALU.add).then_inc(s_sobel, 1)
                dve.wait_ge(*emptied(t, "rows", 2 * NBANK - 1))
                seq(dve.memset(gx[:, 0, :], 0.0))
                seq(dve.memset(gx[:, W - 1, :], 0.0))
                dve.tensor_tensor(gx[:, 1:W - 1, :], along[:, 2:W, :], along[:, 0:W - 2, :], ALU.subtract)\
                   .then_inc(s_sobel, 1)

            def denominator(t):
                A, Bq = arr[2][:, :], arr[3][:, :]
                den, r = arr[0][:, :], arr[1][:, :]
                dve.wait_ge(s_grad2, 2 * t + 2)
                seq(dve.scalar_tensor_tensor(den, A, 1.0, Bq, ALU.add, ALU.mult))
                seq(dve.scalar_tensor_tensor(r, A, 3.5, Bq, ALU.mult, ALU.add))
                seq(dve.scalar_tensor_tensor(den, den, 2.5, r, ALU.mult, ALU.add))
                dve.tensor_scalar(den, den, 4.5, None, ALU.add).then_inc(s_den, 1)

            def diffusion(t):
                A, Bq = arr[2][:, :], arr[3][:, :]
                den, r = arr[0][:, :], arr[1][:, :]
                dve.wait_ge(s_seed, t + 1)
                seq(dve.tensor_tensor(den, den, r, ALU.mult))
                seq(dve.scalar_tensor_tensor(r, den, 2.0, r, ALU.subtract, ALU.mult, reverse0=True))
                seq(dve.scalar_tensor_tensor(Bq, Bq, 1.0, r, ALU.add, ALU.mult))
                seq(dve.scalar_tensor_tensor(A, A, 1.0, r, ALU.add, ALU.mult))
                dve.tensor_tensor(arr[0][:, :], A, Bq, ALU.add).then_inc(s_pq, 1)

            def forcing(t):
                dve.wait_ge(s_pq, t + 1)
                seq(dve.tensor_scalar(arr[1][:, :], arr[0][:, :], -1.0, 1.0, ALU.mult, ALU.add))
                seq(dve.scalar_tensor_tensor(wc(arr[5][:, :]), wc(arr[1][:, :]), 2.0 * DT, inner(h_pad[0]),
                                             ALU.mult, ALU.mult))

            def gate_banks(t, first):
                for q in range(first, first + 2):
                    dve.wait_ge(s_bank, full(t, "conv", q))
                    both = bank(t, "conv", q).rearrange("p (w g c) -> p w g c", g=2, c=C)
                    for g, dst in enumerate((gx_pad, h_pad[1])):
                        cols = both.shape[1]
                        ins = dve.tensor_tensor(
                            dst[:, 1 + q * cols:1 + (q + 1) * cols, 1:C + 1], both[:, :, g, :],
                            bn_shift[:, g, :].unsqueeze(1).to_broadcast([P, cols, C]), ALU.add)
                        if g == 1:
                            ins.then_inc(s_dve, 1)

            def transport_x(t):
                D, DAx = arr[1][:, :], arr[0][:, :]
                dve.wait_ge(s_gates, 2 * t + 1)
                dve.wait_ge(s_c0, t + 1)
                seq(dve.tensor_tensor(wc(DAx), wc(D), inner(gx_pad), ALU.mult))
                seq(dve.tensor_tensor(arr[3][:, :], arr[3][:, :], DAx, ALU.subtract))
                seq(dve.scalar_tensor_tensor(DAx, DAx, 2.0, arr[3][:, :], ALU.mult, ALU.add))

            def transport_y(t):
                D, ay = arr[1][:, :], h_pad[1]
                dve.wait_ge(s_gates, 2 * t + 2)
                for q in range(NBANK):
                    dve.wait_ge(s_bank, full(t, "own", q))
                    cols = slice(q * BANK, (q + 1) * BANK)
                    dve.tensor_tensor(arr[6][:, cols], bank(t, "own", q), D[:, cols], ALU.mult).then_inc(s_dve, 1)
                dve.wait_ge(*emptied(t, "own", NBANK - 1))
                seq(dve.tensor_tensor(wc(D), wc(D), inner(ay), ALU.mult))
                seq(dve.tensor_tensor(arr[2][:, :], arr[2][:, :], D, ALU.subtract))
                seq(dve.scalar_tensor_tensor(D, D, 2.0, arr[2][:, :], ALU.mult, ALU.add))

            def chunk_products(t, it, q):
                n = (t * STEPS + it) * NBANK + q
                h, h0 = h_pad[it % 2], h_pad[0 if it == 0 else (it + 1) % 2]
                c = (it + q) % NBANK
                a, b = c * CHUNK_W, (c + 1) * CHUNK_W
                flat_cols = slice(c * BANK, (c + 1) * BANK)
                kept = rest[:, n % 2, :].rearrange("p (w c) -> p w c", c=C)
                k = it * NBANK + q
                if k >= 2:
                    dve.wait_ge(*emptied(t, "pde", k - 2))
                seq(dve.tensor_tensor(kept, wc(arr[4][:, :])[:, a:b, :], h0[:, a + 1:b + 1, 1:C + 1], ALU.mult))
                dve.tensor_tensor(rest[:, n % 2, :], rest[:, n % 2, :], arr[5][:, flat_cols], ALU.add).then_inc(s_rest, 1)
                if it:
                    dve.wait_ge(s_hhalo, (t * (STEPS - 1) + it - 1) * NBANK + (3 if q == 0 else 4))
                for j, (coef, w0, c0) in enumerate(((6, 1, 1), (2, 1, 0), (1, 1, 2), (3, 0, 1), (0, 2, 1))):
                    m = n * PRODS + j
                    if m >= SLOTS:
                        pn, pj = divmod(m - SLOTS, PRODS)
                        if pj == PRODS - 1:
                            pt, pc = divmod(pn, STEPS * NBANK)
                            dve.wait_ge(s_bank, full(pt, "pde", pc))
                        else:
                            dve.wait_ge(s_summed, pn * (PRODS - 1) + pj + 1)
                    dve.tensor_tensor(prod[:, m % SLOTS, :].rearrange("p (w c) -> p w c", c=C),
                                      wc(arr[coef][:, :])[:, a:b, :],
                                      h[:, a + w0:b + w0, c0:c0 + C], ALU.mult).then_inc(s_prod, 1)

            def chunk_end(t, it, q):
                n = (t * STEPS + it) * NBANK + q
                c = (it + q) % NBANK
                dst = h_pad[(it + 1) % 2]
                dve.wait_ge(s_bank, full(t, "pde", it * NBANK + q))
                dve.wait_ge(s_rest, n + 1)
                dve.tensor_tensor(dst[:, c * CHUNK_W + 1:(c + 1) * CHUNK_W + 1, 1:C + 1],
                                  bank(t, "pde", it * NBANK + q).rearrange("p (w c) -> p w c", c=C),
                                  rest[:, n % 2, :].rearrange("p (w c) -> p w c", c=C), ALU.add).then_inc(s_dve, 1)

            def add_conv(t):
                dve.wait_ge(*emptied(t, "pde", STEPS * NBANK - 1))
                y = wc(arr[0][:, :])
                row = [P, W, C]
                seq(dve.tensor_tensor(y, inner(h_pad[STEPS % 2]), bn_scale[:, 2, :].unsqueeze(1).to_broadcast(row), ALU.mult))
                seq(dve.tensor_tensor(y, y, bn_shift[:, 2, :].unsqueeze(1).to_broadcast(row), ALU.add))
                seq(dve.scalar_tensor_tensor(x1[t][:, :], arr[0][:, :], 0.0, x1[t][:, :], ALU.max, ALU.add))

            def sampling(t, q):
                n, n9 = QCOLS * 2 * K2, QCOLS * K2
                z = arr[1][:, q * QCOLS * OFFS:(q + 1) * QCOLS * OFFS].rearrange("p (w o) -> p w o", o=OFFS)
                dve.wait_ge(s_bank, full(t, "offback", q))
                if t == 0 and q == 0:
                    dve.wait_ge(s_offb, 16)
                dve.tensor_tensor(z, bank(t, "offback", q)[:, 0:QCOLS * OFFP].rearrange("p (w o) -> p w o", o=OFFP)[:, :, 0:OFFS],
                                  off_b[:, :].unsqueeze(1).to_broadcast([P, QCOLS, OFFS]), ALU.add).then_inc(s_dve, 1)
                dve.wait_ge(*emptied(t, "offback", q))

                def wo(a):
                    return a.rearrange("p (w o) -> p w o", o=2 * K2)

                def wk(a):
                    return a.rearrange("p (w k) -> p w k", k=K2)

                pos, low, above = arr[3][:, 0:n], arr[4][:, 0:n], arr[5][:, 0:n]
                seq(dve.tensor_tensor(wo(pos), z[:, :, 0:2 * K2], base_pos[:, q * QCOLS:(q + 1) * QCOLS, :], ALU.add))
                seq(dve.tensor_scalar(pos, pos, CLIP_LOW, CLIP_HIGH, ALU.max, ALU.min))
                seq(dve.tensor_copy(pos_int[:, 0:n], pos))
                seq(dve.tensor_copy(low, pos_int[:, 0:n]))
                seq(dve.tensor_tensor(above, low, pos, ALU.is_gt))
                seq(dve.tensor_tensor(low, low, above, ALU.subtract))
                entry = above[:, 0:n9]
                seq(dve.scalar_tensor_tensor(wk(entry), wo(low)[:, :, 0:K2], float(TX), wo(low)[:, :, K2:2 * K2],
                                             ALU.mult, ALU.add))
                at = t * W * K2 + q * n9
                dve.tensor_scalar(index[:, at:at + n9], entry, const[:, C_ENT + t:C_ENT + t + 1], None,
                                  ALU.add).then_inc(s_index, 1)
                seq(dve.tensor_tensor(pos, pos, low, ALU.subtract))
                dy, dx = wo(pos)[:, :, 0:K2], wo(pos)[:, :, K2:2 * K2]
                mask, bottom, top = arr[2][:, q * n9:(q + 1) * n9], arr[0][:, 0:n9], arr[0][:, n9:2 * n9]
                corner = corner_w[:, t, q * QCOLS:(q + 1) * QCOLS, :].rearrange("p w (k j) -> p w k j", j=4)
                dve.wait_ge(s_mask, QUARTERS * t + q + 1)
                dve.wait_ge(s_cleared, 16 * B)
                seq(dve.tensor_tensor(wk(bottom), wk(mask), dy, ALU.mult))
                seq(dve.tensor_tensor(top, mask, bottom, ALU.subtract))
                seq(dve.tensor_tensor(corner[:, :, :, 3], wk(bottom), dx, ALU.mult))
                seq(dve.tensor_tensor(corner[:, :, :, 2], wk(bottom), corner[:, :, :, 3], ALU.subtract))
                seq(dve.tensor_tensor(corner[:, :, :, 1], wk(top), dx, ALU.mult))
                seq(dve.tensor_tensor(corner[:, :, :, 0], wk(top), corner[:, :, :, 1], ALU.subtract))

            def piece(t, name, i=0):
                which, i = i, int(i) if str(i).isdigit() else 0
                x_t, xn1, xn2 = wc(x1[t][:, :]), wc(xn_flat), xn_pad[:, 1:W + 1, :]
                if name == "sum1":
                    if t == 0:
                        dve.memset(corner_w[:, 0, :, :], 0.0).then_inc(s_zeros, 1)
                    dve.wait_ge(s_x[t], 16)
                    row_sums(x_t)
                elif name == "centre1":
                    if t:
                        dve.wait_ge(s_table, 16 * 2 * IMGS * t)
                    norm_mean(t, 0, x_t, xn1)
                elif name == "square1":
                    dve.wait_ge(s_square, 2 * t + 1)
                    row_sums(wc(flat(h_pad[0])[:, 0:WC]))
                elif name == "deviation1":
                    norm_variance(t, 1)
                elif name == "scale1":
                    norm_scale(2 * t, xn1, s_xn)
                elif name == "rows":
                    if t == 0:
                        parameters()
                elif name == "sobel":
                    sobel(t)
                elif name == "denominator":
                    denominator(t)
                elif name == "gates":
                    dve.wait_ge(s_halo, t + 1)
                    gate_banks(t, 2 * i)
                elif name == "coefficients":
                    diffusion(t)
                elif name == "forcing":
                    forcing(t)
                elif name == "transport":
                    (transport_x if which == "x" else transport_y)(t)
                elif name == "pde":
                    chunk_products(t, *divmod(i, NBANK))
                    if i:
                        chunk_end(t, *divmod(i - 1, NBANK))
                elif name == "add":
                    chunk_end(t, STEPS - 1, NBANK - 1)
                    add_conv(t)
                elif name == "sum2":
                    row_sums(x_t)
                elif name == "centre2":
                    seq(dve.memset(xn_pad[:, 0, :], 0.0))
                    seq(dve.memset(xn_pad[:, W + 1, :], 0.0))
                    norm_mean(t, 2, x_t, xn2)
                elif name == "square2":
                    dve.wait_ge(s_square, 2 * t + 2)
                    row_sums(wc(arr[0][:, :]))
                elif name == "deviation2":
                    norm_variance(t, 3)
                elif name == "scale2":
                    norm_scale(2 * t + 1, xn2, s_xn2)
                elif name == "sampling":
                    sampling(t, i)

            def add_group(t, g, odd=None):
                dve.wait_ge(s_out, (g + (t * GATHER_GROUPS + 1)) * COLS)
                here = x1[t][:, bass.ds(g * (COLS * C), COLS * C)]
                dve.tensor_tensor(here, out_ps[parity(g, odd)], here, ALU.add).then_inc(s_x2, 1)

            def column(t, g, j, odd=None):
                big = g + t * GATHER_GROUPS
                px = pixels[:, j, :, :]
                quads = px.rearrange("p k (q c) -> p (k q) c", c=C)
                dve.wait_ge(s_pixels[j], big * (16 * K2) + 16 * K2)
                weights = corner_w[:, t, :, :].rearrange("p w k -> p (w k)")[
                    :, bass.ds(g * (COLS * 4 * K2) + j * 4 * K2, 4 * K2)]
                dve.tensor_tensor(quads, quads, weights.unsqueeze(2).to_broadcast([P, 4 * K2, C]), ALU.mult)\
                   .then_inc(s_weighted, 1)
                dve.wait_ge(s_weighted, big * COLS + (j + 1))
                dve.tensor_tensor(px[:, :, 0:2 * C], px[:, :, 0:2 * C], px[:, :, 2 * C:4 * C], ALU.add)\
                   .then_inc(s_halved, 1)
                if j == 1:
                    if isinstance(g, int) and g == 0:
                        if t:
                            add_group(t - 1, GATHER_GROUPS - 1)
                    else:
                        add_group(t, g + -1, None if odd is None else 1 - odd)

            dve.memset(one[:, :], 1.0).then_inc(s_part, COLS * PARTS)

            in_order(dve, piece, column)
            add_group(TILES - 1, GATHER_GROUPS - 1)

        @block.scalar
        def _(act):
            steps = [0]

            def seq(ins):
                steps[0] += 1
                ins.then_inc(s_a, 1)
                act.wait_ge(s_a, steps[0])

            def norm_squares(n, centred, square):
                act.wait_ge(s_centred, n + 1)
                act.activation(wc(square), centred, ACT.Square).then_inc(s_square, 1)

            def norm_root(n):
                act.wait_ge(s_ve, n + 1)
                act.activation(grstd[:, :], gvar[:, :], ACT.Sqrt).then_inc(s_sd, 1)

            def channel_halo(h, a, b):
                act.activation(h[:, a + 1:b + 1, 0:1], h[:, a + 1:b + 1, C:C + 1], ACT.Copy)
                return act.activation(h[:, a + 1:b + 1, C + 1:C + 2], h[:, a + 1:b + 1, 1:2], ACT.Copy)

            def column_halo(h, right):
                to, of = (W + 1, 1) if right else (0, W)
                return act.activation(h[:, to, 1:C + 1], h[:, of, 1:C + 1], ACT.Copy)

            def turn_banks(t, what):
                def rows(a):
                    return a.rearrange("p (w h) -> p w h", h=H)

                for q in range(NBANK):
                    act.wait_ge(s_bank, full(t, what, q))
                    if q == 0:
                        for a, h in ((xT[0], 0), (xT[2], H - 1)):
                            act.activation(rows(a)[:, :, h], eye[:, 0:WC // H], ACT.Copy, scale=0.0)
                    src = rows(bank(t, what, q))
                    above, same, below = (rows(a[:, q * BANK:(q + 1) * BANK]) for a in xT)
                    act.activation(same, src, ACT.Copy)
                    act.activation(above[:, :, 1:H], src[:, :, 0:H - 1], ACT.Copy)
                    act.activation(below[:, :, 0:H - 1], src[:, :, 1:H], ACT.Copy).then_inc(s_act, 1)

            def offsets_out(t, q):
                act.wait_ge(s_bank, full(t, "off", q))
                act.activation(arr[6][0:2 * OFFP, q * BANK:(q + 1) * BANK], bank(t, "off", q)[0:2 * OFFP, :],
                               ACT.Copy).then_inc(s_act, 1)

            def masks(t, q):
                act.wait_ge(*emptied(t, "offback", q))
                z = arr[1][:, q * QCOLS * OFFS:(q + 1) * QCOLS * OFFS].rearrange("p (w o) -> p w o", o=OFFS)
                act.activation(arr[2][:, q * QCOLS * K2:(q + 1) * QCOLS * K2].rearrange("p (w k) -> p w k", k=K2),
                               z[:, :, 2 * K2:OFFS], ACT.Sigmoid).then_inc(s_mask, 1)

            def chunk_halo(t, it, q):
                c = (it + q) % NBANK
                h = h_pad[(it + 1) % 2]
                act.wait_ge(*emptied(t, "pde", it * NBANK + q))
                if c == 0:
                    column_halo(h, True)
                if c == NBANK - 1:
                    column_halo(h, False)
                channel_halo(h, c * CHUNK_W, (c + 1) * CHUNK_W).then_inc(s_hhalo, 1)

            def piece(t, name, i=0):
                if name == "centre1":
                    norm_squares(2 * t, wc(xn_flat), flat(h_pad[0])[:, 0:WC])
                elif name == "deviation1":
                    norm_root(2 * t)
                    if t == 0:
                        act.wait_ge(s_bn_ve, 1)
                        act.activation(bn_scale[:, :, :], bn[:, 3, :, :], ACT.Sqrt).then_inc(s_bn_sd, 1)
                elif name in ("turn", "turn2"):
                    turn_banks(t, name)
                elif name == "rows":
                    for q in range(2 * NBANK):
                        act.wait_ge(s_bank, full(t, "rows", q))
                        act.activation(arr[q // NBANK][:, q % NBANK * BANK:(q % NBANK + 1) * BANK],
                                       bank(t, "rows", q), ACT.Copy).then_inc(s_act, 1)
                    seq(act.activation(inner(h_pad[0]), wc(xn_flat), ACT.Copy))
                    column_halo(h_pad[0], True)
                    column_halo(h_pad[0], False)
                    channel_halo(h_pad[0], 0, W).then_inc(s_halo, 1)
                elif name == "sobel":
                    for k in range(2):
                        act.wait_ge(s_sobel, 2 * t + k + 1)
                        act.activation(arr[2 + k][:, :], arr[2 + k][:, :], ACT.Square, scale=0.5).then_inc(s_grad2, 1)
                elif name == "denominator":
                    act.wait_ge(s_den, t + 1)
                    seq(act.activation(arr[1][:, :], arr[0][:, :], ACT.Ln))
                    act.activation(arr[1][:, :], arr[1][:, :], ACT.Exp, scale=-1.0).then_inc(s_seed, 1)
                elif name == "coefficients":
                    act.wait_ge(s_pq, t + 1)
                    act.activation(arr[4][:, :], arr[0][:, :], ACT.Identity, bias=one[:, 0:1], scale=-2.0)\
                       .then_inc(s_c0, 1)
                elif name == "transport" and i == "x":
                    act.wait_ge(*emptied(t, "conv", 2 * NBANK - 1))
                    seq(act.activation(inner(gx_pad), inner(gx_pad), ACT.Relu))
                    column_halo(gx_pad, True)
                    column_halo(gx_pad, False).then_inc(s_gates, 1)
                    seq(act.activation(inner(h_pad[1]), inner(h_pad[1]), ACT.Relu))
                    channel_halo(h_pad[1], 0, W).then_inc(s_gates, 1)
                elif name == "pde":
                    if 0 < int(i) <= (STEPS - 1) * NBANK:
                        chunk_halo(t, *divmod(int(i) - 1, NBANK))
                elif name == "centre2":
                    norm_squares(2 * t + 1, xn_pad[:, 1:W + 1, :], arr[0][:, :])
                elif name == "deviation2":
                    norm_root(2 * t + 1)
                elif name == "offsets":
                    offsets_out(t, int(i))
                elif name == "sampling":
                    masks(t, int(i))

            def column(t, g, j, odd=None):
                big = g + t * GATHER_GROUPS
                col = big * COLS + j
                if not (isinstance(g, int) and big * COLS + j < 2):
                    act.wait_ge(s_out, col - 1)
                for r in range(PARTS):
                    act.wait_ge(s_part, col * PARTS + (r + 1 + COLS * PARTS))
                    act.activation(sampled_T[:, j % 2, r * PART * P:(r + 1) * PART * P],
                                   turned[:, (j * PARTS + r) % PART_SLOTS, 0:PART * P], ACT.Copy).then_inc(s_sT, 1)

            in_order(act, piece, column)

        @block.tensor
        def _(pe):
            def group_sums(t, k):
                pe.wait_ge(s_rsum, NORM_SUMS * t + k + 1)
                if t == 0 and k == 0:
                    pe.wait_ge(s_const, 16)
                wait_bank_empty(pe, t, "sum", k)
                pe.matmul(bank(t, "sum", k)[:, 0:C], ones_block, rsum[:, :], start=True, stop=True).then_inc(s_bank, 1)

            def turn(t, what, src):
                for q in range(NBANK):
                    wait_bank_empty(pe, t, what, q)
                    for i in range(PAIRS_BANK):
                        pair = q * PAIRS_BANK + i
                        ins = pe.transpose(bank(t, what, q)[:, i * P:(i + 1) * P], src[:, pair * P:(pair + 1) * P], eye)
                    ins.then_inc(s_bank, 1)

            def turned_pair(dh, pair):
                return xT[dh][:, pair * P:(pair + 1) * P]

            def depthwise(t, first):
                per_bank = BANK // (4 * C)
                for q in range(first, first + 2):
                    wait_bank_empty(pe, t, "conv", q)
                    for i in range(per_bank):
                        pair = q * per_bank + i
                        dst = bank(t, "conv", q)[:, i * 4 * C:(i + 1) * 4 * C]
                        for dh in range(3):
                            w3 = conv_w[:, dh, :, :].rearrange("p a b -> p (a b)")
                            ins = pe.matmul(dst, turned_pair(dh, pair), w3[:, 0:4 * C], start=dh == 0, stop=False)
                            if pair > 0:
                                ins = pe.matmul(dst[:, 0:2 * C], turned_pair(dh, pair - 1), w3[:, 4 * C:6 * C],
                                                start=False, stop=dh == 2 and pair == PAIRS - 1)
                            if pair < PAIRS - 1:
                                ins = pe.matmul(dst[:, 2 * C:4 * C], turned_pair(dh, pair + 1), w3[:, 6 * C:8 * C],
                                                start=False, stop=dh == 2)
                    ins.then_inc(s_bank, 1)

            def offsets(t, q):
                pe.wait_ge(*emptied(t, "turn2", min(q + 1, NBANK - 1)))
                wait_bank_empty(pe, t, "off", q)
                dst = bank(t, "off", q)[0:2 * OFFP, :]
                a, b = q * BANK, (q + 1) * BANK
                for dh in range(3):
                    pe.matmul(dst, off_w[:, dh, 0, :], xT[dh][:, a:b], start=dh == 0, stop=False)
                    skip = P if q == 0 else 0
                    pe.matmul(dst[:, skip:BANK], off_w[:, dh, 1, :], xT[dh][:, a - P + skip:b - P],
                              start=False, stop=False)
                    skip = P if q == QUARTERS - 1 else 0
                    ins = pe.matmul(dst[:, 0:BANK - skip], off_w[:, dh, 2, :], xT[dh][:, a + P:b + P - skip],
                                    start=False, stop=dh == 2)
                ins.then_inc(s_bank, 1)

            def offsets_back(t, q):
                pe.wait_ge(*emptied(t, "off", q))
                wait_bank_empty(pe, t, "offback", q)
                for i in range(PAIRS_BANK):
                    ins = pe.transpose(bank(t, "offback", q)[:, i * 2 * OFFP:(i + 1) * 2 * OFFP],
                                       arr[6][0:2 * OFFP, q * BANK + i * P:q * BANK + (i + 1) * P],
                                       eye[0:2 * OFFP, 0:2 * OFFP])
                ins.then_inc(s_bank, 1)

            def piece(t, name, i=0):
                if name in ("sum1", "square1", "sum2", "square2"):
                    group_sums(t, ("sum1", "square1", "sum2", "square2").index(name))
                elif name == "turn":
                    pe.wait_ge(s_xn, t + 1)
                    turn(t, "turn", xn_flat)
                elif name == "rows":
                    for q in range(2 * NBANK):
                        wait_bank_empty(pe, t, "rows", q)
                        pe.matmul(bank(t, "rows", q), diff_h if q < NBANK else smooth_h,
                                  xn_flat[:, q % NBANK * BANK:(q % NBANK + 1) * BANK],
                                  start=True, stop=True).then_inc(s_bank, 1)
                elif name == "conv":
                    if t == 0 and i == "0":
                        pe.wait_ge(s_conv_w, 1)
                    pe.wait_ge(*emptied(t, "turn", NBANK - 1))
                    depthwise(t, 2 * int(i))
                elif name == "transport" and i == "x":
                    pe.wait_ge(s_gates, 2 * t + 2)
                    for q in range(NBANK):
                        wait_bank_empty(pe, t, "own", q)
                        a, b = q * CHUNK_W, (q + 1) * CHUNK_W
                        dst = bank(t, "own", q)
                        pe.matmul(dst, eye, gx_pad[:, a + 2:b + 2, 1:C + 1], start=True, stop=False)
                        pe.matmul(dst, minus_eye, gx_pad[:, a:b, 1:C + 1], start=False, stop=False)
                        pe.matmul(dst, eye, h_pad[1][:, a + 1:b + 1, 2:C + 2], start=False, stop=False)
                        pe.matmul(dst, minus_eye, h_pad[1][:, a + 1:b + 1, 0:C], start=False, stop=True)\
                          .then_inc(s_bank, 1)
                elif name == "pde":
                    i = int(i)
                    n = t * STEPS * NBANK + i
                    wait_bank_empty(pe, t, "pde", i)
                    for j in range(PRODS):
                        m = n * PRODS + j
                        pe.wait_ge(s_prod, m + 1)
                        pe.matmul(bank(t, "pde", i), eye, prod[:, m % SLOTS, :], start=j == 0, stop=j == PRODS - 1)\
                          .then_inc(s_bank if j == PRODS - 1 else s_summed, 1)
                elif name == "turn2":
                    pe.wait_ge(s_xn2, t + 1)
                    turn(t, "turn2", scratch[:, C:C + WC])
                elif name == "offsets":
                    if t == 0 and i == "0":
                        pe.wait_ge(s_offw, 16)
                    offsets(t, int(i))
                    offsets_back(t, int(i))

            def turn_part(first, col, j, r):
                if not (first and j * PARTS + r < PART_SLOTS):
                    pe.wait_ge(s_sT, col * PARTS + (r - (PART_SLOTS - 1)))
                for i in range(PART):
                    ins = pe.transpose(turned[:, (j * PARTS + r) % PART_SLOTS, i * P:(i + 1) * P],
                                       pixels[:, j, r * PART + i, 0:2 * C], eye)
                ins.then_inc(s_part, 1)

            def filtered(col, j, out):
                pe.wait_ge(s_sT, (col + 1) * PARTS)
                for k in range(K2):
                    ins = pe.matmul(out[:, j * C:(j + 1) * C], sampled_T[:, j % 2, k * P:(k + 1) * P],
                                    filt[:, k, :], start=k == 0, stop=k == K2 - 1)
                ins.then_inc(s_out, 1)

            def column(t, g, j, odd=None):
                big = g + t * GATHER_GROUPS
                known = isinstance(g, int)
                first = known and big == 0
                if first and j == 0:
                    pe.wait_ge(s_filt, 32)
                col = big * COLS + j
                out = out_ps[parity(g, odd)]
                pe.wait_ge(s_halved, col + 1)
                for r in range(PARTS):
                    turn_part(first, col, j, r)
                if j == 1 and not (known and big < 2):
                    pe.wait_ge(s_x2, big - 1)
                if j:
                    filtered(col - 1, j - 1, out)
                elif not first:
                    filtered(col - 1, COLS - 1, out_ps[1 - parity(g, odd)])

            in_order(pe, piece, column)
            filtered(TILES * W - 1, COLS - 1, out_ps[(GATHER_GROUPS - 1) % 2])


def constants():
    row = np.arange(P)
    h = row % H
    image = row // H
    c = np.zeros((P, C_ALL), np.float32)
    c[:, C_EYE:C_EYE + P] = np.eye(P)
    c[:, C_NEG:C_NEG + P] = -np.eye(P)
    same = image[:, None] == image[None, :]
    c[:, C_ONES:C_ONES + P] = same
    for m in range(P):
        first = m - h[m]
        below = h[m] + 1 if h[m] < H - 1 else H - 2
        above = h[m] - 1 if h[m] > 0 else 1
        c[first + below, C_DIFF + m] += 1
        c[first + above, C_DIFF + m] -= 1
        c[first + below, C_SMOOTH + m] += 1
        c[m, C_SMOOTH + m] += 2
        c[first + above, C_SMOOTH + m] += 1
    c[:, C_MASK:C_MASK + C] = (row % C)[:, None] == np.arange(C)[None, :]
    k = np.arange(K2)
    base = np.zeros((P, W, 2 * K2), np.float32)
    base[:, :, 0:K2] = h[:, None, None] - 1 + (k // 3)[None, None, :]
    base[:, :, K2:] = np.arange(W)[None, :, None] - 1 + (k % 3)[None, None, :]
    c[:, C_BASE:C_ENT] = base.reshape(P, -1)
    for t in range(TILES):
        c[:, C_ENT + t] = (t * IMGS + image) * TY * TX + LO * TX + LO
    return c


def by_parity(w):
    none = np.zeros_like(w[:, 0])
    even = np.stack([w[:, 1], w[:, 0], none, w[:, 2]], 0)
    odd = np.stack([w[:, 2], w[:, 1], w[:, 0], none], 0)
    both = np.stack([even, odd], 0)
    return both.transpose(0, 3, 2, 1, 4).reshape(P, 3, 4, -1)


def stationary(blocks):
    blocks = np.pad(blocks, ((0, 0), (0, 0), (0, 0), (0, OFFP - OFFS)))
    none = np.zeros_like(blocks[:, :, 0])
    parts = [blocks[:, :, 0], blocks[:, :, 1], blocks[:, :, 2], none, none, blocks[:, :, 3]]
    return np.ascontiguousarray(np.stack(parts, 2).reshape(P, -1))


def kernel(x, L0_conv_wg, L0_conv_wg1, L0_conv_g_gamma, L0_conv_g_beta, L0_conv_g_mean, L0_conv_g_var,
           L0_conv_g1_gamma, L0_conv_g1_beta, L0_conv_g1_mean, L0_conv_g1_var, L0_conv_out_gamma,
           L0_conv_out_beta, L0_conv_out_mean, L0_conv_out_var, L1_conv_w_offset, L1_conv_b_offset,
           L1_conv_filt):
    import concourse.bacc as bacc
    from concourse.bass_utils import run_bass_kernel_spmd

    bn = np.stack([L0_conv_g_gamma, L0_conv_g1_gamma, L0_conv_out_gamma,
                   L0_conv_g_beta, L0_conv_g1_beta, L0_conv_out_beta,
                   L0_conv_g_mean, L0_conv_g1_mean, L0_conv_out_mean,
                   L0_conv_g_var, L0_conv_g1_var, L0_conv_out_var], 0)
    arrays = {
        "x_in": np.ascontiguousarray(np.asarray(x).reshape(TILES * P, WC)),
        "taps_in": np.ascontiguousarray(by_parity(np.stack([np.asarray(L0_conv_wg), np.asarray(L0_conv_wg1)], -1))
                                        .reshape(P, -1)),
        "offw_in": stationary(by_parity(np.asarray(L1_conv_w_offset))),
        "filt_in": np.ascontiguousarray(np.asarray(L1_conv_filt).transpose(1, 2, 3, 0).reshape(C, K2 * C)),
        "bn_in": np.ascontiguousarray(bn.reshape(1, 12 * C)),
        "offb_in": np.ascontiguousarray(np.asarray(L1_conv_b_offset).reshape(1, OFFS)),
        "const_in": constants(),
    }
    nc = bacc.Bacc("TRN2", target_bir_lowering=False, num_devices=1)
    args = [nc.dram_tensor(n, a.shape, mybir.dt.from_np(a.dtype), kind="ExternalInput").ap()
            for n, a in arrays.items()]
    out = nc.dram_tensor("out_dram", [TILES * P, WC], mybir.dt.float32, kind="ExternalOutput").ap()
    build_program(nc, *args, out)
    r = run_bass_kernel_spmd(nc, [arrays], core_ids=[0])
    return r.results[0]["out_dram"].reshape(B, H, W, C)
```

```python
import concourse.bass as bass
from concourse import mybir
from contextlib import ExitStack
import numpy as np

B, H, W, C = 8, 32, 32, 64
P = 128
IMGS = P // H
TILES = B // IMGS
WC = W * C
GROUP_SIZE = 2
GROUPS = C // GROUP_SIZE
K2 = 9
OFFS = 3 * K2
DT, BN_EPS, GN_EPS = 0.2, 0.001, 1e-05
STEPS = 5
LO = 2
TY = TX = H + LO + 1
ENTRY = 4 * C
ENTRIES = B * TY * TX
CLIP_LOW, CLIP_HIGH = -float(LO), H + 0.5
BANK = 512
NBANK = WC // BANK
CHUNK_W = BANK // C
PAIRS = W // 2
PAIRS_BANK = PAIRS // NBANK
QUARTERS = NBANK
QCOLS = W // QUARTERS
OFFP = 32
COLS = 4
GATHER_GROUPS = W // COLS
TAP_PAIRS = (K2 + 1) // 2
PARTS = ((0, 3), (3, TAP_PAIRS))
ACT_TAPS = 3
PRODS = 5
SLOTS = 6


def source_on_pe(t, k):
    return t == 1 or k % 4 == 1


C_EYE, C_ONES, C_DIFF, C_SMOOTH, C_MASK, C_NEG, C_BASE = 0, 128, 256, 384, 512, 576, 704
C_ENT = C_BASE + W * 2 * K2
C_ALL = C_ENT + TILES
MAKES = {"sum1": [("sum", 0, "dve")], "square1": [("sum", 1, "dve")], "sum2": [("sum", 2, "dve")],
         "square2": [("sum", 3, "dve")], "turn": [("turn", q, "act") for q in range(NBANK)],
         "rows": [("rows", q, "act") for q in range(2 * NBANK)],
         "own sums": [("own", q, "dve") for q in range(NBANK)],
         "turn2": [("turn2", q, "act") for q in range(NBANK)]}
MAKES.update({f"conv {i}": [("conv", q, "dve") for q in (2 * i, 2 * i + 1)] for i in range(4)})
MAKES.update({f"pde {q}": [("pde", q, "dve")] for q in range(STEPS * NBANK)})
MAKES.update({f"offsets {q}": [("off", q, "act"), ("offback", q, "dve")] for q in range(QUARTERS)})
SCHEDULE = [
    (0, "sum1, centre1, square1, deviation1, scale1, turn, rows, sobel, denominator, conv 0, gates 0, conv 1, "
        "coefficients, gates 1, conv 2, conv 3, forcing, gates 2"),
    (1, "sum1"),
    (0, "gates 3, relu"),
    (1, "centre1"),
    (0, "own sums, transport x"),
    (1, "square1"),
    (0, "transport y, own"),
    (1, "deviation1"),
    (0, "pde 0, pde 1, pde 2, pde 3, pde 4, pde 5, pde 6, pde 7, pde 8, pde 9, pde 10, pde 11, pde 12, pde 13, "
        "pde 14, pde 15, pde 16, pde 17, pde 18, pde 19, add, sum2, centre2, square2, deviation2, scale2, "
        "turn2"),
    (1, "scale1"),
    (0, "offsets 0, offsets 1, sampling 0, offsets 2, sampling 1, offsets 3, sampling 2, weigh column"),
    (1, "turn, rows, turn column, conv 0, sobel, copy column, weigh column, column, denominator, conv 1, "
        "gates 0, weigh column, copy column, gates 1, coefficients, copy column, turn column, conv 2, "
        "turn column, forcing, gates 2, conv 3, column, gates 3, relu, weigh column, scale 6, turn column, "
        "copy column, own sums, scale 7, copy column, transport x, turn column, transport y, scale 8, column, "
        "weigh column, copy column, own, scale 9, pde 0, column, pde 1, scale 10, turn column, weigh column, "
        "pde 2, pde 3, scale 11, column, pde 4, scale 12, pde 5, column, pde 6, pde 7, pde 8, pde 9, pde 10, "
        "scale 13, turn column, copy column, weigh column, scale 14, scale 15, pde 11, column, pde 12, "
        "scale 16, column, column, pde 13, scale 17, column, pde 14, scale 18, column, pde 15, pde 16, "
        "scale 19, scale 20, scale 21, pde 17, weigh column, pde 18, column, pde 19, column, add, column, "
        "sum2, weigh column, centre2, square2, turn column, scale 23, turn column, copy column, scale 24, "
        "turn column, weigh column, deviation2, copy column, scale2, turn2, copy column, weigh column, "
        "offsets 0, copy column, turn column, offsets 1, weigh column, copy column, turn column, weigh column, "
        "column, turn column, copy column, column, sampling 0, offsets 2, offsets 3, weigh column, scale 30, "
        "turn column, copy column, sampling 2, copy column, turn column, turn column, weigh column, "
        "copy column, weigh column"),
]
COLUMN = ("weigh column", "turn column", "copy column")
ORDER = [(0 if "column" in part or part.startswith("scale ") else tile, part)
         for tile, pieces in SCHEDULE for piece in pieces.split(", ")
         for part in (COLUMN if piece == "column" else (piece,))]
PLAN = [(t,) + made for t, piece in ORDER for made in MAKES.get(piece, [])]
AT = {made[:3]: n for n, made in enumerate(PLAN)}


def build_program(nc, x_in, taps_in, offw_in, filt_in, bn_in, offb_in, const_in, out_dram):
    f32, i32, u32 = mybir.dt.float32, mybir.dt.int32, mybir.dt.uint32
    ALU, ACT, AX = mybir.AluOpType, mybir.ActivationFunctionType, mybir.AxisListType
    table = nc.dram_tensor("table", [ENTRIES, ENTRY], f32, kind="Internal").ap()
    table_y = table.rearrange("(b y x) e -> b y x e", b=B, y=TY)

    with ExitStack() as ctx:
        def sb(name, shape, dt=f32):
            return ctx.enter_context(nc.sbuf_tensor(name, shape, dt))

        def psum(name, shape):
            return ctx.enter_context(nc.psum_tensor(name, shape, f32))

        def sem(name):
            return ctx.enter_context(nc.semaphore(name))

        const = sb("const", [P, C_ALL])
        eye = const[:, C_EYE:C_EYE + P]
        ones_block = const[:, C_ONES:C_ONES + P]
        diff_h = const[:, C_DIFF:C_DIFF + P]
        smooth_h = const[:, C_SMOOTH:C_SMOOTH + P]
        minus_eye = const[:, C_NEG:C_NEG + P]
        same_c = const[:, C_MASK:C_MASK + C]
        base_pos = const[:, C_BASE:C_ENT].rearrange("p (w o) -> p w o", o=2 * K2)
        taps = sb("taps", [P, 3, 4, 2])
        conv_w = sb("conv_w", [P, 3, 4, 2 * C])
        off_w = sb("off_w", [P, 3, 3, 2 * OFFP])
        filt = sb("filt", [P, TAP_PAIRS, C])
        off_b = sb("off_b", [P, OFFS])
        xn_next = sb("xn_next", [P, WC])
        bn = xn_next[:, 0:4 * 3 * C].rearrange("p (a b c) -> p a b c", b=3, c=C)
        bn_scale = sb("bn_scale", [P, 3, C])
        bn_shift = sb("bn_shift", [P, 3, C])
        x1 = [sb(f"x1_{t}", [P, WC]) for t in range(TILES)]
        h_pad = [sb(f"h_pad{i}", [P, W + 2, C + 2]) for i in range(2)]
        scratch = sb("scratch", [P, (W + 2) * (C + 2)])
        xn_flat = (scratch[:, 0:WC], xn_next[:, :])
        gx_pad = scratch[:, :].rearrange("p (w c) -> p w c", c=C + 2)
        xn_pad = scratch[:, 0:(W + 2) * C].rearrange("p (w c) -> p w c", c=C)
        arrays = sb("arrays", [P, 8, WC])
        arr = {name: arrays[:, place, :] for place, name in enumerate((3, 0, 1, 2, "mid", 4, 5, 6))}
        xT_mid = arr["mid"]
        shared = sb("shared", [P, 2 * WC])
        xT = (shared[:, 0:WC], xT_mid[:, :], shared[:, WC:2 * WC])
        prod = shared[:, 0:SLOTS * BANK].rearrange("p (s n) -> p s n", n=BANK)
        rest = shared[:, SLOTS * BANK:(SLOTS + 2) * BANK].rearrange("p (s n) -> p s n", n=BANK)
        rsum = sb("rsum", [P, C])
        gmean = sb("gmean", [P, GROUPS])
        gvar = sb("gvar", [P, TILES, GROUPS])
        grstd = sb("grstd", [P, TILES, GROUPS])
        gtmp = sb("gtmp", [P, GROUPS])
        one = sb("one", [P, 1])
        den_const = sb("den_const", [P, 1])
        pos_int = sb("pos_int", [P, 2 * QCOLS * 2 * K2], i32)
        corner_w = sb("corner_w", [P, TILES, W, K2 * 4])
        index = sb("index", [P, TILES * W * K2], u32)
        index_now = sb("index_now", [P, 2, QCOLS, K2], u32)
        pixels = sb("pixels", [P, COLS, K2, ENTRY])
        squares = pixels[:, :, :, :].rearrange("p a b c -> p (a b c)")[:, 0:WC]
        sampled_T = sb("sampled_T", [P, 2, TAP_PAIRS * P])
        sums = sb("sums", [P, 2, TAP_PAIRS * P])
        acc = psum("acc", [P, NBANK, BANK])
        side = psum("side", [P, NBANK, BANK])
        turned = side[:, 0:len(PARTS), :]
        out_ps = [side[:, 2, 0:COLS * C], side[:, 3, 0:COLS * C]]

        s_const, s_taps, s_offw, s_filt, s_bn, s_offb = (
            sem(n) for n in ("const_in", "taps_in", "offw_in", "filt_in", "bn_in", "offb_in"))
        s_x = [sem(f"x_in{t}") for t in range(TILES)]
        s_zeros = sem("zeros_ready")
        s_cleared = sem("table_cleared")
        s_table = sem("table_written")
        s_conv_w = sem("conv_w_ready")
        s_bn_ve = sem("bn_var_eps_ready")
        s_bn_sd = sem("bn_sd_ready")
        s_rsum = sem("row_sums_ready")
        s_centred = sem("centred_ready")
        s_square = sem("squares_ready")
        s_ve = sem("var_eps_ready")
        s_sd = sem("sd_ready")
        s_xn = sem("xn_ready")
        s_halo = sem("xn_halo_ready")
        s_bank = sem("bank_full")
        s_act = sem("bank_emptied_by_act")
        s_dve = sem("bank_emptied_by_dve")
        s_sobel = sem("gradient_ready")
        s_grad2 = sem("squared_gradients_ready")
        s_den = sem("denominator_ready")
        s_seed = sem("reciprocal_seed_ready")
        s_pq = sem("p_plus_q_ready")
        s_c0 = sem("c0_ready")
        s_d = sem("d_ready")
        s_gates = sem("gates_ready")
        s_prod = sem("product_ready")
        s_summed = sem("product_summed")
        s_rest = sem("rest_ready")
        s_hhalo = sem("h_halo_ready")
        s_xn2 = sem("xn2_ready")
        s_mask = sem("mask_ready")
        s_index = sem("index_ready")
        s_corners = sem("corner_weights_ready")
        s_copied = sem("indices_copied")
        s_begun = sem("column_begun")
        s_pixels = [sem(f"pixels_in{j}") for j in range(COLS)]
        s_halved = sem("halved_ready")
        s_sums = sem("column_summed")
        s_part = sem("part_turned")
        s_sT = sem("sampled_T_ready")
        s_weighted = sem("weighted")
        s_scaled = sem("scaled_by_act")
        s_out = sem("column_filtered")
        s_x2 = sem("group_added")
        s_store = sem("stored")
        s_v = sem("vector_step")
        s_a = sem("scalar_step")

        block = ctx.enter_context(nc.Block())

        def flat(a):
            return a.rearrange("p w c -> p (w c)")

        def wc(a):
            return a.rearrange("p (w c) -> p w c", c=C)

        def inner(a):
            return a[:, 1:W + 1, 1:C + 1]

        def emptied(t, what, q):
            n = AT[t, what, q]
            who = PLAN[n][3]
            return {"act": s_act, "dve": s_dve}[who], [p[3] for p in PLAN[:n + 1]].count(who)

        def full(t, what, q):
            return AT[t, what, q] + 1

        def bank(t, what, q):
            return acc[:, AT[t, what, q] % NBANK, :]

        def wait_bank_empty(pe, t, what, q):
            n = AT[t, what, q] - NBANK
            if n >= 0:
                pe.wait_ge(*emptied(*PLAN[n][:3]))

        def scaled(w):
            return (0, f"scale {w}") in ORDER

        def scaled_until(w):
            return [scaled(v) for v in range(w + 1)].count(True)

        def in_order(eng, part, piece, column):
            done = 0
            for t, name in ORDER:
                if name == part:
                    column(0, done // COLS, done % COLS)
                    done += 1
                elif not name.endswith(" column"):
                    piece(t, *name.split())
            for j in range(COLS):
                column(1, 0, j)
            with eng.Fori(0, GATHER_GROUPS // 2 - 1, 1) as i:
                for odd in (1, 0):
                    for j in range(COLS):
                        column(1, i * 2 + (2 - odd), j, odd)
            for j in range(COLS):
                column(1, GATHER_GROUPS - 1, j)

        def prod_slot(n, j):
            return PRODS - 1 + n % 2 if j == 0 else j - 1

        def chunk_bank(n):
            return n // (STEPS * NBANK), "pde", n % (STEPS * NBANK)

        def norm_index(t, which):
            return (which - 1) * TILES + t

        def parity(g, odd):
            return g % 2 if odd is None else odd

        @block.sync
        def _(sp):
            sp.dma_start(x1[0][:, :], x_in[0:P, :]).then_inc(s_x[0], 16)
            sp.dma_start(const[:, :], const_in).then_inc(s_const, 16)
            sp.dma_start(xn_next[:, 0:4 * 3 * C],
                         bn_in.to_broadcast([P, 12 * C])).then_inc(s_bn, 16)
            sp.dma_start(taps[:, :, :, :].rearrange("p a b c -> p (a b c)"), taps_in).then_inc(s_taps, 16)
            sp.dma_start(off_w[:, :, :, :].rearrange("p a b c -> p (a b c)"), offw_in).then_inc(s_offw, 16)
            sp.dma_start(filt[:, :, :].rearrange("p k f -> p (k f)"), filt_in).then_inc(s_filt, 16)
            sp.dma_start(off_b[:, :], offb_in.to_broadcast([P, OFFS])).then_inc(s_offb, 16)
            sp.dma_start(x1[1][:, :], x_in[P:2 * P, :]).then_inc(s_x[1], 16)
            sp.wait_ge(s_zeros, 1)
            for b in range(B):
                sp.dma_start(table[b * TY * TX:(b + 1) * TY * TX, :].rearrange("(y x) e -> y x e", y=TY),
                             corner_w[0:TY, :, :, :].rearrange("p t w k -> p (t w k)")[:, 0:ENTRY]
                             .unsqueeze(1).to_broadcast([TY, TX, ENTRY])).then_inc(s_cleared, 16)
            sp.wait_ge(s_cleared, 16 * B)
            for t in range(TILES):
                sp.wait_ge(s_xn2, t + 1)
                for i in range(IMGS):
                    rows = scratch[i * H:(i + 1) * H, 0:(W + 1) * C].rearrange("p (w c) -> p w c", c=C)
                    pairs = bass.AP(tensor=rows.tensor, offset=rows.offset,
                                    ap=[list(rows.ap[0]), [C, W + 1], [1, 2 * C]])
                    for half in range(2):
                        sp.dma_start(table_y[t * IMGS + i, LO - half:LO - half + H, 1:W + 2,
                                             half * 2 * C:(half + 1) * 2 * C], pairs).then_inc(s_table, 16)
            for t in range(TILES):
                with sp.Fori(0, GATHER_GROUPS, 1) as g:
                    sp.wait_ge(s_x2, g + (t * GATHER_GROUPS + 1))
                    sp.dma_start(out_dram[t * P:(t + 1) * P, bass.ds(g * (COLS * C), COLS * C)],
                                 x1[t][:, bass.ds(g * (COLS * C), COLS * C)]).then_inc(s_store, 16)
            sp.wait_ge(s_store, 16 * TILES * GATHER_GROUPS)

        @block.gpsimd
        def _(pool):
            for t in range(TILES):
                pool.wait_ge(s_table, 16 * 2 * IMGS * (t + 1))
                with pool.Fori(0, QUARTERS // 2, 1) as i:
                    for odd in range(2):
                        q = i * 2 + (t * QUARTERS + odd)
                        pool.wait_ge(s_index, q + 1)
                        pool.tensor_copy(index_now[:, odd, :, :].rearrange("p j k -> p (j k)"),
                                         index[:, bass.ds(q * (QCOLS * K2), QCOLS * K2)]).then_inc(s_copied, 1)
                        pool.wait_ge(s_copied, q + 1)
                        for w in range(QCOLS):
                            pool.wait_ge(s_sums, q * QCOLS + (w + 1))
                            pool.sem_inc(s_begun, 1)
                            for k in range(K2):
                                pool.indirect_dma_start(
                                    out=pixels[:, w % COLS, k, :], out_offset=None, in_=table,
                                    in_offset=bass.IndirectOffsetOnAxis(ap=index_now[:, odd, w, k:k + 1], axis=0),
                                ).then_inc(s_pixels[w % COLS], 16)

        @block.vector
        def _(dve):
            steps = [0]

            def seq(ins):
                steps[0] += 1
                ins.then_inc(s_v, 1)
                dve.wait_ge(s_v, steps[0])

            def per_group(a):
                return a.unsqueeze(1).unsqueeze(3).to_broadcast([P, W, GROUPS, GROUP_SIZE])

            def grouped(a):
                return a.rearrange("p w (g j) -> p w g j", j=GROUP_SIZE)

            def rsqrt_refined(root, v, tmp):
                seq(dve.reciprocal(root, root))
                seq(dve.tensor_tensor(tmp, root, root, ALU.mult))
                seq(dve.tensor_tensor(tmp, tmp, v, ALU.mult))
                seq(dve.tensor_scalar(tmp, tmp, -0.5, 1.5, ALU.mult, ALU.add))
                seq(dve.tensor_tensor(root, root, tmp, ALU.mult))

            def norm_mean(t, k, src, dst):
                dve.wait_ge(s_bank, full(t, "sum", k))
                dve.tensor_reduce(gmean[:, :], bank(t, "sum", k)[:, 0:C].rearrange("p (g j) -> p g j", j=GROUP_SIZE),
                                  AX.X, ALU.add).then_inc(s_dve, 1)
                dve.wait_ge(*emptied(t, "sum", k))
                seq(dve.tensor_scalar(gmean[:, :], gmean[:, :], 1.0 / (H * W * GROUP_SIZE), None, ALU.mult))
                dve.tensor_tensor(grouped(dst), grouped(src), per_group(gmean[:, :]), ALU.subtract)\
                   .then_inc(s_centred, 1)

            def norm_variance(t, k):
                dve.wait_ge(s_bank, full(t, "sum", k))
                dve.tensor_reduce(gvar[:, t, :], bank(t, "sum", k)[:, 0:C].rearrange("p (g j) -> p g j", j=GROUP_SIZE),
                                  AX.X, ALU.add).then_inc(s_dve, 1)
                dve.wait_ge(*emptied(t, "sum", k))
                dve.tensor_scalar(gvar[:, t, :], gvar[:, t, :], 1.0 / (H * W * GROUP_SIZE), GN_EPS, ALU.mult, ALU.add)\
                   .then_inc(s_ve, 1)

            def norm_scale(t, n, dst, ready):
                dve.wait_ge(s_sd, n + 1)
                rsqrt_refined(grstd[:, t, :], gvar[:, t, :], gtmp[:, :])
                dve.tensor_tensor(grouped(dst), grouped(dst), per_group(grstd[:, t, :]), ALU.mult).then_inc(ready, 1)

            def row_sums(a):
                dve.tensor_reduce(rsum[:, :], a.rearrange("p w c -> p c w"), AX.X, ALU.add).then_inc(s_rsum, 1)

            def parameters():
                dve.wait_ge(s_bn, 16)
                gamma, beta, mean, var = (bn[:, i, :, :] for i in range(4))
                dve.tensor_scalar(var, var, BN_EPS, None, ALU.add).then_inc(s_bn_ve, 1)
                dve.wait_ge(s_bn_sd, 1)
                rsqrt_refined(bn_scale[:, :, :], var, bn_shift[:, :, :])
                seq(dve.tensor_tensor(bn_scale[:, :, :], bn_scale[:, :, :], gamma, ALU.mult))
                seq(dve.tensor_tensor(bn_shift[:, :, :], bn_scale[:, :, :], mean, ALU.mult))
                seq(dve.tensor_tensor(bn_shift[:, :, :], beta, bn_shift[:, :, :], ALU.subtract))
                seq(dve.tensor_scalar(bn_scale[:, 0:2, :], bn_scale[:, 0:2, :], DT, None, ALU.mult))
                seq(dve.tensor_scalar(bn_shift[:, 0:2, :], bn_shift[:, 0:2, :], DT, None, ALU.mult))
                dve.wait_ge(s_const, 16)
                dve.wait_ge(s_taps, 16)
                cells = conv_w[:, :, :, :].rearrange("p a b (g c) -> p (a b g) c", c=C)
                seq(dve.tensor_tensor(cells, same_c.unsqueeze(1).to_broadcast([P, 24, C]),
                                      taps[:, :, :, :].rearrange("p a b g -> p (a b g)").unsqueeze(2)
                                      .to_broadcast([P, 24, C]), ALU.mult))
                rows = conv_w[:, :, :, :].rearrange("p a b c -> p (a b) c")
                dve.tensor_tensor(rows, rows, bn_scale[:, 0:2, :].rearrange("p g c -> p (g c)").unsqueeze(1)
                                  .to_broadcast([P, 12, 2 * C]), ALU.mult).then_inc(s_conv_w, 1)

            def sobel(t):
                across, along = wc(arr[0][:, :]), wc(arr[1][:, :])
                gy, gx = wc(arr[2][:, :]), wc(arr[3][:, :])
                dve.wait_ge(*emptied(t, "rows", NBANK - 1))
                seq(dve.tensor_tensor(gy[:, 1:W - 1, :], across[:, 0:W - 2, :], across[:, 2:W, :], ALU.add))
                seq(dve.tensor_scalar(gy[:, 0, :], across[:, 1, :], 2.0, None, ALU.mult))
                seq(dve.tensor_scalar(gy[:, W - 1, :], across[:, W - 2, :], 2.0, None, ALU.mult))
                dve.scalar_tensor_tensor(gy, across, 2.0, gy, ALU.mult, ALU.add).then_inc(s_sobel, 1)
                dve.wait_ge(*emptied(t, "rows", 2 * NBANK - 1))
                seq(dve.memset(gx[:, 0, :], 0.0))
                seq(dve.memset(gx[:, W - 1, :], 0.0))
                dve.tensor_tensor(gx[:, 1:W - 1, :], along[:, 2:W, :], along[:, 0:W - 2, :], ALU.subtract)\
                   .then_inc(s_sobel, 1)

            def denominator(t):
                A, Bq = arr[2][:, :], arr[3][:, :]
                den, r = arr[0][:, :], arr[1][:, :]
                dve.wait_ge(s_grad2, 2 * t + 2)
                seq(dve.scalar_tensor_tensor(den, A, 1.0, Bq, ALU.add, ALU.mult))
                seq(dve.scalar_tensor_tensor(r, A, 3.5, Bq, ALU.mult, ALU.add))
                dve.scalar_tensor_tensor(den, den, 2.5, r, ALU.mult, ALU.add).then_inc(s_den, 1)

            def diffusion(t):
                A, Bq = arr[2][:, :], arr[3][:, :]
                den, r = arr[0][:, :], arr[1][:, :]
                dve.wait_ge(s_seed, t + 1)
                seq(dve.scalar_tensor_tensor(den, den, 4.5, r, ALU.add, ALU.mult))
                seq(dve.scalar_tensor_tensor(r, den, 2.0, r, ALU.subtract, ALU.mult, reverse0=True))
                seq(dve.scalar_tensor_tensor(Bq, Bq, 1.0, r, ALU.add, ALU.mult))
                seq(dve.scalar_tensor_tensor(A, A, 1.0, r, ALU.add, ALU.mult))
                dve.tensor_tensor(arr[0][:, :], A, Bq, ALU.add).then_inc(s_pq, 1)

            def forcing(t):
                dve.wait_ge(s_d, t + 1)
                seq(dve.scalar_tensor_tensor(wc(arr[5][:, :]), wc(arr[1][:, :]), 2.0 * DT, inner(h_pad[0]),
                                             ALU.mult, ALU.mult))

            def gate_banks(t, first):
                for q in range(first, first + 2):
                    dve.wait_ge(s_bank, full(t, "conv", q))
                    both = bank(t, "conv", q).rearrange("p (w g c) -> p w g c", g=2, c=C)
                    for g, dst in enumerate((gx_pad, h_pad[1])):
                        cols = both.shape[1]
                        ins = dve.tensor_tensor(
                            dst[:, 1 + q * cols:1 + (q + 1) * cols, 1:C + 1], both[:, :, g, :],
                            bn_shift[:, g, :].unsqueeze(1).to_broadcast([P, cols, C]), ALU.add)
                        if g == 1:
                            ins.then_inc(s_dve, 1)

            def transport_x(t):
                D, DAx = arr[1][:, :], arr[0][:, :]
                dve.wait_ge(s_gates, 2 * t + 1)
                dve.wait_ge(s_c0, t + 1)
                seq(dve.tensor_tensor(wc(DAx), wc(D), inner(gx_pad), ALU.mult))
                seq(dve.tensor_tensor(arr[3][:, :], arr[3][:, :], DAx, ALU.subtract))
                seq(dve.scalar_tensor_tensor(DAx, DAx, 2.0, arr[3][:, :], ALU.mult, ALU.add))

            def transport_y(t):
                D, DAy, ay = arr[1][:, :], xT_mid[:, :], h_pad[1]
                dve.wait_ge(s_gates, 2 * t + 2)
                seq(dve.tensor_tensor(wc(DAy), wc(D), inner(ay), ALU.mult))
                seq(dve.tensor_tensor(arr[2][:, :], arr[2][:, :], DAy, ALU.subtract))
                seq(dve.scalar_tensor_tensor(DAy, DAy, 2.0, arr[2][:, :], ALU.mult, ALU.add))

            def own_banks(t):
                for q in range(NBANK):
                    dve.wait_ge(s_bank, full(t, "own", q))
                    cols = slice(q * BANK, (q + 1) * BANK)
                    dve.tensor_tensor(arr[6][:, cols], bank(t, "own", q), arr[1][:, cols], ALU.mult).then_inc(s_dve, 1)
                dve.wait_ge(*emptied(t, "own", NBANK - 1))

            def two(a, b):
                return bass.AP(tensor=a.tensor, offset=a.offset,
                               ap=[list(a.ap[0]), [b.offset - a.offset, 2]] + [list(d) for d in a.ap[1:]])

            def chunk_products(t, it, q):
                n = (t * STEPS + it) * NBANK + q
                h, h0 = h_pad[it % 2], h_pad[0 if it == 0 else (it + 1) % 2]
                c = (it + q) % NBANK
                a, b = c * CHUNK_W, (c + 1) * CHUNK_W
                flat_cols = slice(c * BANK, (c + 1) * BANK)
                kept = rest[:, n % 2, :].rearrange("p (w c) -> p w c", c=C)
                k = it * NBANK + q
                if k >= 2:
                    dve.wait_ge(*emptied(t, "pde", k - 2))
                ins = dve.tensor_tensor(kept, wc(arr[4][:, :])[:, a:b, :], h0[:, a + 1:b + 1, 1:C + 1], ALU.mult)
                if source_on_pe(t, k):
                    ins.then_inc(s_rest, 1)
                else:
                    seq(ins)
                    dve.tensor_tensor(rest[:, n % 2, :], rest[:, n % 2, :], arr[5][:, flat_cols], ALU.add)\
                       .then_inc(s_rest, 1)
                if it:
                    dve.wait_ge(s_hhalo, (t * (STEPS - 1) + it - 1) * NBANK + (3 if q == 0 else 4))

                def coef(name):
                    return wc(arr[name])[:, a:b, :]

                def moved(dw, dc):
                    return h[:, a + 1 + dw:b + 1 + dw, 1 + dc:1 + dc + C]

                if n >= 2:
                    dve.wait_ge(s_summed, (n - 2) * (PRODS - 1) + 1)
                dve.tensor_tensor(wc(prod[:, prod_slot(n, 0), :]), coef(6), moved(0, 0), ALU.mult).then_inc(s_prod, 1)
                if n:
                    dve.wait_ge(s_summed, (n - 1) * (PRODS - 1) + 3)
                dve.tensor_tensor(two(wc(prod[:, prod_slot(n, 1), :]), wc(prod[:, prod_slot(n, 2), :])),
                                  two(coef(2), coef("mid")), two(moved(0, -1), moved(0, 1)), ALU.mult)\
                   .then_inc(s_prod, 2)
                if n:
                    dve.wait_ge(s_bank, full(*chunk_bank(n - 1)))
                dve.tensor_tensor(two(wc(prod[:, prod_slot(n, 3), :]), wc(prod[:, prod_slot(n, 4), :])),
                                  two(coef(3), coef(0)), two(moved(-1, 0), moved(1, 0)), ALU.mult)\
                   .then_inc(s_prod, 2)

            def chunk_end(t, it, q):
                n = (t * STEPS + it) * NBANK + q
                c = (it + q) % NBANK
                dst = h_pad[(it + 1) % 2]
                dve.wait_ge(s_bank, full(t, "pde", it * NBANK + q))
                dve.wait_ge(s_rest, n + 1)
                dve.tensor_tensor(dst[:, c * CHUNK_W + 1:(c + 1) * CHUNK_W + 1, 1:C + 1],
                                  bank(t, "pde", it * NBANK + q).rearrange("p (w c) -> p w c", c=C),
                                  rest[:, n % 2, :].rearrange("p (w c) -> p w c", c=C), ALU.add).then_inc(s_dve, 1)

            def add_conv(t):
                dve.wait_ge(*emptied(t, "pde", STEPS * NBANK - 1))
                y = wc(arr[0][:, :])
                row = [P, W, C]
                seq(dve.tensor_tensor(y, inner(h_pad[STEPS % 2]), bn_scale[:, 2, :].unsqueeze(1).to_broadcast(row),
                                      ALU.mult))
                seq(dve.tensor_tensor(y, y, bn_shift[:, 2, :].unsqueeze(1).to_broadcast(row), ALU.add))
                seq(dve.scalar_tensor_tensor(x1[t][:, :], arr[0][:, :], 0.0, x1[t][:, :], ALU.max, ALU.add))

            def sampling(t, q, number):
                cols = number * QCOLS
                n, n9 = cols * 2 * K2, cols * K2
                z = arr[1][:, q * QCOLS * OFFS:(q + number) * QCOLS * OFFS].rearrange("p (w o) -> p w o", o=OFFS)
                for k in range(number):
                    dve.wait_ge(s_bank, full(t, "offback", q + k))
                    if t == 0 and q == 0:
                        dve.wait_ge(s_offb, 16)
                    dve.tensor_tensor(z[:, k * QCOLS:(k + 1) * QCOLS, :],
                                      bank(t, "offback", q + k)[:, 0:QCOLS * OFFP]
                                      .rearrange("p (w o) -> p w o", o=OFFP)[:, :, 0:OFFS],
                                      off_b[:, :].unsqueeze(1).to_broadcast([P, QCOLS, OFFS]), ALU.add)\
                       .then_inc(s_dve, 1)
                dve.wait_ge(*emptied(t, "offback", q + number - 1))

                def wo(a):
                    return a.rearrange("p (w o) -> p w o", o=2 * K2)

                def wk(a):
                    return a.rearrange("p (w k) -> p w k", k=K2)

                pos, low, above = arr[3][:, 0:n], arr[4][:, 0:n], arr[5][:, 0:n]
                seq(dve.tensor_tensor(wo(pos), z[:, :, 0:2 * K2], base_pos[:, q * QCOLS:q * QCOLS + cols, :], ALU.add))
                seq(dve.tensor_scalar(pos, pos, CLIP_LOW, CLIP_HIGH, ALU.max, ALU.min))
                seq(dve.tensor_copy(pos_int[:, 0:n], pos))
                seq(dve.tensor_copy(low, pos_int[:, 0:n]))
                seq(dve.tensor_tensor(above, low, pos, ALU.is_gt))
                seq(dve.tensor_tensor(low, low, above, ALU.subtract))
                entry = above[:, 0:n9]
                seq(dve.scalar_tensor_tensor(wk(entry), wo(low)[:, :, 0:K2], float(TX), wo(low)[:, :, K2:2 * K2],
                                             ALU.mult, ALU.add))
                at = (t * W + q * QCOLS) * K2
                dve.tensor_scalar(index[:, at:at + n9], entry, const[:, C_ENT + t:C_ENT + t + 1], None,
                                  ALU.add).then_inc(s_index, number)
                seq(dve.tensor_tensor(pos, pos, low, ALU.subtract))
                dy, dx = wo(pos)[:, :, 0:K2], wo(pos)[:, :, K2:2 * K2]
                mask, bottom, top = arr[2][:, q * QCOLS * K2:q * QCOLS * K2 + n9], arr[0][:, 0:n9], arr[0][:, n9:2 * n9]
                corner = corner_w[:, t, q * QCOLS:q * QCOLS + cols, :].rearrange("p w (k j) -> p w k j", j=4)
                dve.wait_ge(s_mask, QUARTERS * t + q + number)
                dve.wait_ge(s_cleared, 16 * B)
                seq(dve.tensor_tensor(wk(bottom), wk(mask), dy, ALU.mult))
                seq(dve.tensor_tensor(top, mask, bottom, ALU.subtract))
                seq(dve.tensor_tensor(corner[:, :, :, 3], wk(bottom), dx, ALU.mult))
                seq(dve.tensor_tensor(corner[:, :, :, 2], wk(bottom), corner[:, :, :, 3], ALU.subtract))
                seq(dve.tensor_tensor(corner[:, :, :, 1], wk(top), dx, ALU.mult))
                dve.tensor_tensor(corner[:, :, :, 0], wk(top), corner[:, :, :, 1], ALU.subtract)\
                   .then_inc(s_corners, number)
                dve.wait_ge(s_corners, t * QUARTERS + q + number)

            def piece(t, name, i=0):
                which, i = i, int(i) if str(i).isdigit() else 0
                x_t, xn1, xn2 = wc(x1[t][:, :]), wc(xn_flat[t]), xn_pad[:, 1:W + 1, :]
                if name == "sum1":
                    if t == 0:
                        dve.memset(corner_w[:, 0, :, :], 0.0).then_inc(s_zeros, 1)
                    dve.wait_ge(s_x[t], 16)
                    row_sums(x_t)
                elif name == "centre1":
                    norm_mean(t, 0, x_t, xn1)
                elif name == "square1":
                    dve.wait_ge(s_square, norm_index(t, 1) + 1)
                    row_sums(wc(squares))
                elif name == "deviation1":
                    norm_variance(t, 1)
                elif name == "scale1":
                    norm_scale(t, norm_index(t, 1), xn1, s_xn)
                elif name == "rows":
                    if t == 0:
                        parameters()
                elif name == "sobel":
                    sobel(t)
                elif name == "denominator":
                    denominator(t)
                elif name == "gates":
                    if t and i == 0:
                        dve.wait_ge(s_table, 16 * 2 * IMGS * t)
                    dve.wait_ge(s_halo, t + 1)
                    gate_banks(t, 2 * i)
                elif name == "coefficients":
                    diffusion(t)
                elif name == "forcing":
                    forcing(t)
                elif name == "transport":
                    (transport_x if which == "x" else transport_y)(t)
                elif name == "own" and which != "sums":
                    own_banks(t)
                elif name == "pde":
                    chunk_products(t, *divmod(i, NBANK))
                    if i:
                        chunk_end(t, *divmod(i - 1, NBANK))
                elif name == "add":
                    chunk_end(t, STEPS - 1, NBANK - 1)
                    add_conv(t)
                elif name == "sum2":
                    row_sums(x_t)
                elif name == "centre2":
                    seq(dve.memset(xn_pad[:, 0, :], 0.0))
                    seq(dve.memset(xn_pad[:, W + 1, :], 0.0))
                    norm_mean(t, 2, x_t, xn2)
                elif name == "square2":
                    dve.wait_ge(s_square, norm_index(t, 2) + 1)
                    row_sums(wc(arr[0][:, :]))
                elif name == "deviation2":
                    norm_variance(t, 3)
                elif name == "scale2":
                    norm_scale(t, norm_index(t, 2), xn2, s_xn2)
                elif name == "sampling":
                    sampling(t, i, 2 if i == 2 or t else 1)

            def add_group(t, g, odd=None):
                dve.wait_ge(s_out, (g + (t * GATHER_GROUPS + 1)) * COLS)
                here = x1[t][:, bass.ds(g * (COLS * C), COLS * C)]
                dve.tensor_tensor(here, out_ps[parity(g, odd)], here, ALU.add).then_inc(s_x2, 1)

            def column(t, g, j, odd=None):
                big = g + t * GATHER_GROUPS
                px = pixels[:, j, :, :]
                quads = px.rearrange("p k (q c) -> p (k q) c", c=C)
                dve.wait_ge(s_pixels[j], big * (16 * K2) + 16 * K2)
                weights = corner_w[:, t, :, :].rearrange("p w k -> p (w k)")[
                    :, bass.ds(g * (COLS * 4 * K2) + j * 4 * K2, 4 * K2)]
                shared_with_act = t == 0 and scaled(g * COLS + j)
                cells = 4 * (K2 - (ACT_TAPS if shared_with_act else 0))
                dve.tensor_tensor(quads[:, 0:cells, :], quads[:, 0:cells, :],
                                  weights[:, 0:cells].unsqueeze(2).to_broadcast([P, cells, C]), ALU.mult)\
                   .then_inc(s_weighted, 1)
                dve.wait_ge(s_weighted, big * COLS + (j + 1))
                if shared_with_act:
                    dve.wait_ge(s_scaled, scaled_until(g * COLS + j))
                dve.tensor_tensor(px[:, :, 0:2 * C], px[:, :, 0:2 * C], px[:, :, 2 * C:4 * C], ALU.add)\
                   .then_inc(s_halved, 1)
                dve.wait_ge(s_halved, big * COLS + (j + 1))
                if not (isinstance(g, int) and big * COLS + j < 2):
                    dve.wait_ge(s_part, (big * COLS + (j - 1)) * len(PARTS))
                dve.tensor_tensor(sums[:, j % 2, 0:K2 * C].rearrange("p (k c) -> p k c", c=C),
                                  px[:, :, 0:C], px[:, :, C:2 * C], ALU.add).then_inc(s_sums, 1)
                if j == 1:
                    if isinstance(g, int) and g == 0:
                        if t:
                            add_group(t - 1, GATHER_GROUPS - 1)
                    else:
                        add_group(t, g + -1, None if odd is None else 1 - odd)

            dve.memset(den_const[:, :], 4.5)
            dve.memset(one[:, :], 1.0).then_inc(s_sums, COLS)
            dve.memset(sums[:, :, K2 * C:TAP_PAIRS * P], 0.0)

            in_order(dve, "weigh column", piece, column)
            add_group(TILES - 1, GATHER_GROUPS - 1)

        @block.scalar
        def _(act):
            steps = [0]

            def seq(ins):
                steps[0] += 1
                ins.then_inc(s_a, 1)
                act.wait_ge(s_a, steps[0])

            def norm_squares(n, centred, square):
                act.wait_ge(s_centred, n + 1)
                act.activation(wc(square), centred, ACT.Square).then_inc(s_square, 1)

            def norm_root(t, n):
                act.wait_ge(s_ve, n + 1)
                act.activation(grstd[:, t, :], gvar[:, t, :], ACT.Sqrt).then_inc(s_sd, 1)

            def channel_halo(h, a, b):
                act.activation(h[:, a + 1:b + 1, 0:1], h[:, a + 1:b + 1, C:C + 1], ACT.Copy)
                return act.activation(h[:, a + 1:b + 1, C + 1:C + 2], h[:, a + 1:b + 1, 1:2], ACT.Copy)

            def column_halo(h, right):
                to, of = (W + 1, 1) if right else (0, W)
                return act.activation(h[:, to, 1:C + 1], h[:, of, 1:C + 1], ACT.Copy)

            def turn_banks(t, what):
                def rows(a):
                    return a.rearrange("p (w h) -> p w h", h=H)

                for q in range(NBANK):
                    act.wait_ge(s_bank, full(t, what, q))
                    if q == 0:
                        for a, h in ((xT[0], 0), (xT[2], H - 1)):
                            act.activation(rows(a)[:, :, h], eye[:, 0:WC // H], ACT.Copy, scale=0.0)
                    src = rows(bank(t, what, q))
                    above, same, below = (rows(a[:, q * BANK:(q + 1) * BANK]) for a in xT)
                    act.activation(same, src, ACT.Copy)
                    act.activation(above[:, :, 1:H], src[:, :, 0:H - 1], ACT.Copy)
                    act.activation(below[:, :, 0:H - 1], src[:, :, 1:H], ACT.Copy).then_inc(s_act, 1)

            def offsets_out(t, q):
                act.wait_ge(s_bank, full(t, "off", q))
                act.activation(arr[6][0:2 * OFFP, q * BANK:(q + 1) * BANK], bank(t, "off", q)[0:2 * OFFP, :],
                               ACT.Copy).then_inc(s_act, 1)

            def masks(t, q):
                act.wait_ge(*emptied(t, "offback", q))
                z = arr[1][:, q * QCOLS * OFFS:(q + 1) * QCOLS * OFFS].rearrange("p (w o) -> p w o", o=OFFS)
                act.activation(arr[2][:, q * QCOLS * K2:(q + 1) * QCOLS * K2].rearrange("p (w k) -> p w k", k=K2),
                               z[:, :, 2 * K2:OFFS], ACT.Sigmoid).then_inc(s_mask, 1)

            def chunk_halo(t, it, q):
                c = (it + q) % NBANK
                h = h_pad[(it + 1) % 2]
                act.wait_ge(*emptied(t, "pde", it * NBANK + q))
                if c == 0:
                    column_halo(h, True)
                if c == NBANK - 1:
                    column_halo(h, False)
                channel_halo(h, c * CHUNK_W, (c + 1) * CHUNK_W).then_inc(s_hhalo, 1)

            def piece(t, name, i=0):
                if name == "centre1":
                    norm_squares(norm_index(t, 1), wc(xn_flat[t]), squares)
                elif name == "deviation1":
                    norm_root(t, norm_index(t, 1))
                    if t == 0:
                        act.wait_ge(s_bn_ve, 1)
                        act.activation(bn_scale[:, :, :], bn[:, 3, :, :], ACT.Sqrt).then_inc(s_bn_sd, 1)
                elif name in ("turn", "turn2"):
                    turn_banks(t, name)
                elif name == "rows":
                    if t:
                        act.wait_ge(s_corners, t * QUARTERS)
                    for q in range(2 * NBANK):
                        act.wait_ge(s_bank, full(t, "rows", q))
                        act.activation(arr[q // NBANK][:, q % NBANK * BANK:(q % NBANK + 1) * BANK],
                                       bank(t, "rows", q), ACT.Copy).then_inc(s_act, 1)
                    seq(act.activation(inner(h_pad[0]), wc(xn_flat[t]), ACT.Copy))
                    column_halo(h_pad[0], True)
                    column_halo(h_pad[0], False)
                    channel_halo(h_pad[0], 0, W).then_inc(s_halo, 1)
                elif name == "sobel":
                    for k in range(2):
                        act.wait_ge(s_sobel, 2 * t + k + 1)
                        act.activation(arr[2 + k][:, :], arr[2 + k][:, :], ACT.Square, scale=0.5).then_inc(s_grad2, 1)
                elif name == "denominator":
                    act.wait_ge(s_den, t + 1)
                    seq(act.activation(arr[1][:, :], arr[0][:, :], ACT.Ln, bias=den_const[:, 0:1]))
                    act.activation(arr[1][:, :], arr[1][:, :], ACT.Exp, scale=-1.0).then_inc(s_seed, 1)
                elif name == "coefficients":
                    act.wait_ge(s_pq, t + 1)
                    act.activation(arr[1][:, :], arr[0][:, :], ACT.Identity, bias=one[:, 0:1], scale=-1.0)\
                       .then_inc(s_d, 1)
                    act.activation(arr[4][:, :], arr[0][:, :], ACT.Identity, bias=one[:, 0:1], scale=-2.0)\
                       .then_inc(s_c0, 1)
                elif name == "relu":
                    act.wait_ge(*emptied(t, "conv", 2 * NBANK - 1))
                    seq(act.activation(inner(gx_pad), inner(gx_pad), ACT.Relu))
                    column_halo(gx_pad, True)
                    column_halo(gx_pad, False).then_inc(s_gates, 1)
                    seq(act.activation(inner(h_pad[1]), inner(h_pad[1]), ACT.Relu))
                    channel_halo(h_pad[1], 0, W).then_inc(s_gates, 1)
                elif name == "pde":
                    if 0 < int(i) <= (STEPS - 1) * NBANK:
                        chunk_halo(t, *divmod(int(i) - 1, NBANK))
                elif name == "centre2":
                    norm_squares(norm_index(t, 2), xn_pad[:, 1:W + 1, :], arr[0][:, :])
                elif name == "deviation2":
                    norm_root(t, norm_index(t, 2))
                elif name == "scale":
                    scale_column(int(i))
                elif name == "offsets":
                    offsets_out(t, int(i))
                elif name == "sampling":
                    for q in range(int(i), int(i) + (2 if i == "2" or t else 1)):
                        masks(t, q)

            def scale_column(w):
                act.wait_ge(s_corners, w // QCOLS + 1)
                act.wait_ge(s_pixels[w % COLS], (w // COLS + 1) * (16 * K2))
                for k in range(K2 - ACT_TAPS, K2):
                    for q in range(4):
                        cell = pixels[:, w % COLS, k, q * C:(q + 1) * C]
                        ins = act.activation(cell, cell, ACT.Copy, scale=corner_w[:, 0, w, 4 * k + q:4 * k + q + 1])
                ins.then_inc(s_scaled, 1)

            def column(t, g, j, odd=None):
                big = g + t * GATHER_GROUPS
                col = big * COLS + j
                if not (isinstance(g, int) and big * COLS + j < 2):
                    act.wait_ge(s_out, col - 1)
                for r, (a, b) in enumerate(PARTS):
                    act.wait_ge(s_part, col * len(PARTS) + (r + 1))
                    act.activation(sampled_T[:, j % 2, a * P:b * P], turned[:, r, 0:(b - a) * P], ACT.Copy)\
                       .then_inc(s_sT, 1)

            in_order(act, "copy column", piece, column)

        @block.tensor
        def _(pe):
            def group_sums(t, k):
                pe.wait_ge(s_rsum, 2 * norm_index(t, k // 2 + 1) + k % 2 + 1)
                if t == 0 and k == 0:
                    pe.wait_ge(s_const, 16)
                wait_bank_empty(pe, t, "sum", k)
                pe.matmul(bank(t, "sum", k)[:, 0:C], ones_block, rsum[:, :], start=True, stop=True).then_inc(s_bank, 1)

            def turn(t, what, src):
                for q in range(NBANK):
                    wait_bank_empty(pe, t, what, q)
                    for i in range(PAIRS_BANK):
                        pair = q * PAIRS_BANK + i
                        ins = pe.transpose(bank(t, what, q)[:, i * P:(i + 1) * P], src[:, pair * P:(pair + 1) * P], eye)
                    ins.then_inc(s_bank, 1)

            def turned_pair(dh, pair):
                return xT[dh][:, pair * P:(pair + 1) * P]

            def depthwise(t, first):
                per_bank = BANK // (4 * C)
                for q in range(first, first + 2):
                    wait_bank_empty(pe, t, "conv", q)
                    for i in range(per_bank):
                        pair = q * per_bank + i
                        dst = bank(t, "conv", q)[:, i * 4 * C:(i + 1) * 4 * C]
                        for dh in range(3):
                            w3 = conv_w[:, dh, :, :].rearrange("p a b -> p (a b)")
                            ins = pe.matmul(dst, turned_pair(dh, pair), w3[:, 0:4 * C], start=dh == 0, stop=False)
                            if pair > 0:
                                ins = pe.matmul(dst[:, 0:2 * C], turned_pair(dh, pair - 1), w3[:, 4 * C:6 * C],
                                                start=False, stop=dh == 2 and pair == PAIRS - 1)
                            if pair < PAIRS - 1:
                                ins = pe.matmul(dst[:, 2 * C:4 * C], turned_pair(dh, pair + 1), w3[:, 6 * C:8 * C],
                                                start=False, stop=dh == 2)
                    ins.then_inc(s_bank, 1)

            def offsets(t, q):
                pe.wait_ge(*emptied(t, "turn2", min(q + 1, NBANK - 1)))
                wait_bank_empty(pe, t, "off", q)
                dst = bank(t, "off", q)[0:2 * OFFP, :]
                a, b = q * BANK, (q + 1) * BANK
                for dh in range(3):
                    pe.matmul(dst, off_w[:, dh, 0, :], xT[dh][:, a:b], start=dh == 0, stop=False)
                    skip = P if q == 0 else 0
                    pe.matmul(dst[:, skip:BANK], off_w[:, dh, 1, :], xT[dh][:, a - P + skip:b - P],
                              start=False, stop=False)
                    skip = P if q == QUARTERS - 1 else 0
                    ins = pe.matmul(dst[:, 0:BANK - skip], off_w[:, dh, 2, :], xT[dh][:, a + P:b + P - skip],
                                    start=False, stop=dh == 2)
                ins.then_inc(s_bank, 1)

            def offsets_back(t, q):
                pe.wait_ge(*emptied(t, "off", q))
                wait_bank_empty(pe, t, "offback", q)
                for i in range(PAIRS_BANK):
                    ins = pe.transpose(bank(t, "offback", q)[:, i * 2 * OFFP:(i + 1) * 2 * OFFP],
                                       arr[6][0:2 * OFFP, q * BANK + i * P:q * BANK + (i + 1) * P],
                                       eye[0:2 * OFFP, 0:2 * OFFP])
                ins.then_inc(s_bank, 1)

            def piece(t, name, i=0):
                if name in ("sum1", "square1", "sum2", "square2"):
                    group_sums(t, ("sum1", "square1", "sum2", "square2").index(name))
                elif name == "turn":
                    pe.wait_ge(s_xn, t + 1)
                    turn(t, "turn", xn_flat[t])
                elif name == "rows":
                    for q in range(2 * NBANK):
                        wait_bank_empty(pe, t, "rows", q)
                        pe.matmul(bank(t, "rows", q), diff_h if q < NBANK else smooth_h,
                                  xn_flat[t][:, q % NBANK * BANK:(q % NBANK + 1) * BANK],
                                  start=True, stop=True).then_inc(s_bank, 1)
                elif name == "conv":
                    if t == 0 and i == "0":
                        pe.wait_ge(s_conv_w, 1)
                    pe.wait_ge(*emptied(t, "turn", NBANK - 1))
                    depthwise(t, 2 * int(i))
                elif name == "own" and i == "sums":
                    pe.wait_ge(s_gates, 2 * t + 2)
                    for q in range(NBANK):
                        wait_bank_empty(pe, t, "own", q)
                        a, b = q * CHUNK_W, (q + 1) * CHUNK_W
                        dst = bank(t, "own", q)
                        pe.matmul(dst, eye, gx_pad[:, a + 2:b + 2, 1:C + 1], start=True, stop=False)
                        pe.matmul(dst, minus_eye, gx_pad[:, a:b, 1:C + 1], start=False, stop=False)
                        pe.matmul(dst, eye, h_pad[1][:, a + 1:b + 1, 2:C + 2], start=False, stop=False)
                        pe.matmul(dst, minus_eye, h_pad[1][:, a + 1:b + 1, 0:C], start=False, stop=True)\
                          .then_inc(s_bank, 1)
                elif name == "pde":
                    i = int(i)
                    n = t * STEPS * NBANK + i
                    wait_bank_empty(pe, t, "pde", i)
                    for j in range(PRODS):
                        m = n * PRODS + j
                        pe.wait_ge(s_prod, m + 1)
                        if j == PRODS - 1 and source_on_pe(t, i):
                            c = (i // NBANK + i) % NBANK
                            pe.matmul(bank(t, "pde", i), eye, arr[5][:, c * BANK:(c + 1) * BANK],
                                      start=False, stop=False)
                        pe.matmul(bank(t, "pde", i), eye, prod[:, prod_slot(n, j), :],
                                  start=j == 0, stop=j == PRODS - 1)\
                          .then_inc(s_bank if j == PRODS - 1 else s_summed, 1)
                elif name == "turn2":
                    pe.wait_ge(s_xn2, t + 1)
                    turn(t, "turn2", scratch[:, C:C + WC])
                elif name == "offsets":
                    if t == 0 and i == "0":
                        pe.wait_ge(s_offw, 16)
                    offsets(t, int(i))
                    offsets_back(t, int(i))

            def turn_part(first, col, j, r):
                if not (first and j == 0):
                    pe.wait_ge(s_sT, col * len(PARTS) + (r + 1 - len(PARTS)))
                a, b = PARTS[r]
                for i in range(a, b):
                    ins = pe.transpose(turned[:, r, (i - a) * P:(i - a + 1) * P],
                                       sums[:, j % 2, i * P:(i + 1) * P], eye)
                ins.then_inc(s_part, 1)

            def filtered(col, j, out):
                pe.wait_ge(s_sT, (col + 1) * len(PARTS))
                for k in range(TAP_PAIRS):
                    ins = pe.matmul(out[:, j * C:(j + 1) * C], sampled_T[:, j % 2, k * P:(k + 1) * P],
                                    filt[:, k, :], start=k == 0, stop=k == TAP_PAIRS - 1)
                ins.then_inc(s_out, 1)

            def column(t, g, j, odd=None):
                big = g + t * GATHER_GROUPS
                known = isinstance(g, int)
                first = known and big == 0
                if first and j == 0:
                    pe.wait_ge(s_filt, 16)
                col = big * COLS + j
                out = out_ps[parity(g, odd)]
                pe.wait_ge(s_sums, col + (1 + COLS))
                for r in range(len(PARTS)):
                    turn_part(first, col, j, r)
                if j == 1 and not (known and big < 2):
                    pe.wait_ge(s_x2, big - 1)
                if j:
                    filtered(col - 1, j - 1, out)
                elif not first:
                    filtered(col - 1, COLS - 1, out_ps[1 - parity(g, odd)])

            in_order(pe, "turn column", piece, column)
            filtered(TILES * W - 1, COLS - 1, out_ps[(GATHER_GROUPS - 1) % 2])


def constants():
    row = np.arange(P)
    h = row % H
    image = row // H
    c = np.zeros((P, C_ALL), np.float32)
    c[:, C_EYE:C_EYE + P] = np.eye(P)
    c[:, C_NEG:C_NEG + P] = -np.eye(P)
    same = image[:, None] == image[None, :]
    c[:, C_ONES:C_ONES + P] = same
    for m in range(P):
        first = m - h[m]
        below = h[m] + 1 if h[m] < H - 1 else H - 2
        above = h[m] - 1 if h[m] > 0 else 1
        c[first + below, C_DIFF + m] += 1
        c[first + above, C_DIFF + m] -= 1
        c[first + below, C_SMOOTH + m] += 1
        c[m, C_SMOOTH + m] += 2
        c[first + above, C_SMOOTH + m] += 1
    c[:, C_MASK:C_MASK + C] = (row % C)[:, None] == np.arange(C)[None, :]
    k = np.arange(K2)
    base = np.zeros((P, W, 2 * K2), np.float32)
    base[:, :, 0:K2] = h[:, None, None] - 1 + (k // 3)[None, None, :]
    base[:, :, K2:] = np.arange(W)[None, :, None] - 1 + (k % 3)[None, None, :]
    c[:, C_BASE:C_ENT] = base.reshape(P, -1)
    for t in range(TILES):
        c[:, C_ENT + t] = (t * IMGS + image) * TY * TX + LO * TX + LO
    return c


def by_parity(w):
    none = np.zeros_like(w[:, 0])
    even = np.stack([w[:, 1], w[:, 0], none, w[:, 2]], 0)
    odd = np.stack([w[:, 2], w[:, 1], w[:, 0], none], 0)
    both = np.stack([even, odd], 0)
    return both.transpose(0, 3, 2, 1, 4).reshape(P, 3, 4, -1)


def stationary(blocks):
    blocks = np.pad(blocks, ((0, 0), (0, 0), (0, 0), (0, OFFP - OFFS)))
    none = np.zeros_like(blocks[:, :, 0])
    parts = [blocks[:, :, 0], blocks[:, :, 1], blocks[:, :, 2], none, none, blocks[:, :, 3]]
    return np.ascontiguousarray(np.stack(parts, 2).reshape(P, -1))


def tap_pairs(filt):
    taps = np.pad(filt.reshape(C, C, K2), ((0, 0), (0, 0), (0, 2 * TAP_PAIRS - K2)))
    return np.ascontiguousarray(taps.reshape(C, C, TAP_PAIRS, 2).transpose(3, 1, 2, 0).reshape(P, -1))


def kernel(x, L0_conv_wg, L0_conv_wg1, L0_conv_g_gamma, L0_conv_g_beta, L0_conv_g_mean, L0_conv_g_var,
           L0_conv_g1_gamma, L0_conv_g1_beta, L0_conv_g1_mean, L0_conv_g1_var, L0_conv_out_gamma,
           L0_conv_out_beta, L0_conv_out_mean, L0_conv_out_var, L1_conv_w_offset, L1_conv_b_offset,
           L1_conv_filt):
    import concourse.bacc as bacc
    from concourse.bass_utils import run_bass_kernel_spmd

    bn = np.stack([L0_conv_g_gamma, L0_conv_g1_gamma, L0_conv_out_gamma,
                   L0_conv_g_beta, L0_conv_g1_beta, L0_conv_out_beta,
                   L0_conv_g_mean, L0_conv_g1_mean, L0_conv_out_mean,
                   L0_conv_g_var, L0_conv_g1_var, L0_conv_out_var], 0)
    arrays = {
        "x_in": np.ascontiguousarray(np.asarray(x).reshape(TILES * P, WC)),
        "taps_in": np.ascontiguousarray(by_parity(np.stack([np.asarray(L0_conv_wg), np.asarray(L0_conv_wg1)], -1))
                                        .reshape(P, -1)),
        "offw_in": stationary(by_parity(np.asarray(L1_conv_w_offset))),
        "filt_in": tap_pairs(np.asarray(L1_conv_filt)),
        "bn_in": np.ascontiguousarray(bn.reshape(1, 12 * C)),
        "offb_in": np.ascontiguousarray(np.asarray(L1_conv_b_offset).reshape(1, OFFS)),
        "const_in": constants(),
    }
    nc = bacc.Bacc("TRN2", target_bir_lowering=False, num_devices=1)
    args = [nc.dram_tensor(n, a.shape, mybir.dt.from_np(a.dtype), kind="ExternalInput").ap()
            for n, a in arrays.items()]
    out = nc.dram_tensor("out_dram", [TILES * P, WC], mybir.dt.float32, kind="ExternalOutput").ap()
    build_program(nc, *args, out)
    r = run_bass_kernel_spmd(nc, [arrays], core_ids=[0])
    return r.results[0]["out_dram"].reshape(B, H, W, C)
```
